# Optimizing a Trainium2 kernel written in Bass

```python
import numpy as np
import jax
import jax.numpy as jnp

def _softmax(x, axis=-1):
    return jax.nn.softmax(x, axis=axis)

def _gelu(x):
    return jax.nn.gelu(x, approximate=True)

def _silu(x):
    return jax.nn.silu(x)

def _sigmoid(x):
    return jax.nn.sigmoid(x)

def _layernorm(x, axis=-1, eps=1e-05):
    m = jnp.mean(x, axis=axis, keepdims=True)
    v = jnp.var(x, axis=axis, keepdims=True)
    return (x - m) / jnp.sqrt(v + eps)

def _scatter_add(tgt, idx, src, axis=0):
    return tgt.at[idx].add(src)

def _segment_sum(src, seg, n):
    return jax.ops.segment_sum(src, seg, n)
kernel_name = 'mk_seq_preln_d1_jaxref_r4_e4cb5b'

def setup_inputs(seed: int=0):
    np.random.seed(seed)
    _w = jnp.asarray

    def _L0_attn_setup():
        import jax, jax.numpy as jnp
        import numpy as np
        LN_EPS = 1e-05
        WKV_EPS = 1e-08

        def _layernorm(x, g, b):
            mu = jnp.mean(x, axis=-1, keepdims=True)
            var = jnp.mean((x - mu) ** 2, axis=-1, keepdims=True)
            return (x - mu) * jax.lax.rsqrt(var + LN_EPS) * g + b

        def _time_mix(xn, Wr, Ww, Wk, Wv, Wo, time_decay):
            r = jax.nn.sigmoid(jnp.einsum('bsd,ed->bse', xn, Wr))
            w = -jnp.exp(jnp.einsum('bsd,ed->bse', xn, Ww))
            k = jnp.einsum('bsd,ed->bse', xn, Wk)
            v = jnp.einsum('bsd,ed->bse', xn, Wv)
            ewk = jnp.exp(w + k)
            decay = jnp.exp(time_decay)

            def step(carry, inp):
                num, den = carry
                e, vt = inp
                num = decay * num + e * vt
                den = decay * den + e
                wkv = num / (den + WKV_EPS)
                return ((num, den), wkv)
            B, S, D = xn.shape
            init = (jnp.zeros((B, D), xn.dtype), jnp.zeros((B, D), xn.dtype))
            (num_f, den_f), wkv = jax.lax.scan(step, init, (jnp.swapaxes(ewk, 0, 1), jnp.swapaxes(v, 0, 1)))
            wkv = jnp.swapaxes(wkv, 0, 1)
            out = jnp.einsum('bsd,ed->bse', r * wkv, Wo)
            final_state = jnp.stack([num_f, den_f], axis=1)
            return (out, final_state)

        def _channel_mix(xn, Wkey, Wval, Wrec):
            k = jnp.einsum('bsd,fd->bsf', xn, Wkey)
            k = jnp.square(jax.nn.relu(k))
            v = jnp.einsum('bsf,df->bsd', k, Wval)
            r = jax.nn.sigmoid(jnp.einsum('bsd,ed->bse', xn, Wrec))
            return r * v

        def _reference_tuple_inner(x, ln1_g, ln1_b, ln2_g, ln2_b, Wr, Ww, Wk, Wv, Wo, time_decay, time_first, Wkey, Wval, Wrec):
            tm, new_state = _time_mix(_layernorm(x, ln1_g, ln1_b), Wr, Ww, Wk, Wv, Wo, time_decay)
            x = x + tm
            x = x + _channel_mix(_layernorm(x, ln2_g, ln2_b), Wkey, Wval, Wrec)
            return (x, new_state)
        key = jax.random.key(seed)
        ks = jax.random.split(key, 16)
        B, S, D, F = (4, 512, 256, 1024)
        xavier_d = float(np.sqrt(6.0 / (D + D)))
        xavier_df = float(np.sqrt(6.0 / (D + F)))
        u = lambda k, sh, s: jax.random.uniform(k, sh, jnp.float32, -s, s)
        return {'x': jax.random.normal(ks[0], (B, S, D), jnp.float32), 'ln1_g': jnp.ones((D,), jnp.float32), 'ln1_b': jnp.zeros((D,), jnp.float32), 'ln2_g': jnp.ones((D,), jnp.float32), 'ln2_b': jnp.zeros((D,), jnp.float32), 'Wr': u(ks[1], (D, D), xavier_d), 'Ww': u(ks[2], (D, D), xavier_d), 'Wk': u(ks[3], (D, D), xavier_d), 'Wv': u(ks[4], (D, D), xavier_d), 'Wo': u(ks[5], (D, D), xavier_d), 'time_decay': jax.random.uniform(ks[6], (D,), jnp.float32, -1.0, 0.0), 'time_first': jax.random.uniform(ks[7], (D,), jnp.float32, -1.0, 1.0), 'Wkey': u(ks[8], (F, D), xavier_df), 'Wval': u(ks[9], (D, F), xavier_df), 'Wrec': u(ks[10], (D, D), xavier_d)}
    _L0_attn_in = _L0_attn_setup()

    def _L0_ffn_setup():
        import jax, jax.numpy as jnp
        import numpy as np
        DMODEL = 256
        N_EXPERTS = 32
        EXPERT_SIZE = 128
        N_HEADS = 4
        WEIGHT_SCALE = 1.0
        key = jax.random.key(seed)
        k0, k1, k2, k3 = jax.random.split(key, 4)
        x = jax.random.normal(k0, (2, 512, DMODEL), dtype=jnp.float32)
        expert_sel = jax.random.normal(k1, (N_EXPERTS, DMODEL), dtype=jnp.float32) * DMODEL ** (-0.5)
        keys = jax.random.normal(k2, (N_EXPERTS, DMODEL, EXPERT_SIZE), dtype=jnp.float32) * DMODEL ** (-0.5)
        values = jax.random.normal(k3, (N_EXPERTS, EXPERT_SIZE, DMODEL), dtype=jnp.float32) * (N_EXPERTS * EXPERT_SIZE) ** (-0.5)
        return {'x': x, 'expert_sel': expert_sel, 'keys': keys, 'values': values}
    _L0_ffn_in = _L0_ffn_setup()
    _d = {'L0_attn_x': _L0_attn_in['x'], 'L0_attn_ln1_g': _L0_attn_in['ln1_g'], 'L0_attn_ln1_b': _L0_attn_in['ln1_b'], 'L0_attn_ln2_g': _L0_attn_in['ln2_g'], 'L0_attn_ln2_b': _L0_attn_in['ln2_b'], 'L0_attn_Wr': _L0_attn_in['Wr'], 'L0_attn_Ww': _L0_attn_in['Ww'], 'L0_attn_Wk': _L0_attn_in['Wk'], 'L0_attn_Wv': _L0_attn_in['Wv'], 'L0_attn_Wo': _L0_attn_in['Wo'], 'L0_attn_time_decay': _L0_attn_in['time_decay'], 'L0_attn_time_first': _L0_attn_in['time_first'], 'L0_attn_Wkey': _L0_attn_in['Wkey'], 'L0_attn_Wval': _L0_attn_in['Wval'], 'L0_attn_Wrec': _L0_attn_in['Wrec'], 'L0_ffn_expert_sel': _L0_ffn_in['expert_sel'], 'L0_ffn_keys': _L0_ffn_in['keys'], 'L0_ffn_values': _L0_ffn_in['values']}
    _x0 = _d['L0_attn_x']
    _d['L0_attn_x'] = jax.random.normal(jax.random.fold_in(jax.random.key(seed), 1), (8, 1024, 256), dtype=_x0.dtype)
    del _x0
    return _d

def reference(L0_attn_x, L0_attn_ln1_g, L0_attn_ln1_b, L0_attn_ln2_g, L0_attn_ln2_b, L0_attn_Wr, L0_attn_Ww, L0_attn_Wk, L0_attn_Wv, L0_attn_Wo, L0_attn_time_decay, L0_attn_time_first, L0_attn_Wkey, L0_attn_Wval, L0_attn_Wrec, L0_ffn_expert_sel, L0_ffn_keys, L0_ffn_values):

    def _L0_attn_ref(x, ln1_g, ln1_b, ln2_g, ln2_b, Wr, Ww, Wk, Wv, Wo, time_decay, time_first, Wkey, Wval, Wrec):
        import jax, jax.numpy as jnp
        import numpy as np
        LN_EPS = 1e-05
        WKV_EPS = 1e-08

        def _layernorm(x, g, b):
            mu = jnp.mean(x, axis=-1, keepdims=True)
            var = jnp.mean((x - mu) ** 2, axis=-1, keepdims=True)
            return (x - mu) * jax.lax.rsqrt(var + LN_EPS) * g + b

        def _time_mix(xn, Wr, Ww, Wk, Wv, Wo, time_decay):
            r = jax.nn.sigmoid(jnp.einsum('bsd,ed->bse', xn, Wr))
            w = -jnp.exp(jnp.einsum('bsd,ed->bse', xn, Ww))
            k = jnp.einsum('bsd,ed->bse', xn, Wk)
            v = jnp.einsum('bsd,ed->bse', xn, Wv)
            ewk = jnp.exp(w + k)
            decay = jnp.exp(time_decay)

            def step(carry, inp):
                num, den = carry
                e, vt = inp
                num = decay * num + e * vt
                den = decay * den + e
                wkv = num / (den + WKV_EPS)
                return ((num, den), wkv)
            B, S, D = xn.shape
            init = (jnp.zeros((B, D), xn.dtype), jnp.zeros((B, D), xn.dtype))
            (num_f, den_f), wkv = jax.lax.scan(step, init, (jnp.swapaxes(ewk, 0, 1), jnp.swapaxes(v, 0, 1)))
            wkv = jnp.swapaxes(wkv, 0, 1)
            out = jnp.einsum('bsd,ed->bse', r * wkv, Wo)
            final_state = jnp.stack([num_f, den_f], axis=1)
            return (out, final_state)

        def _channel_mix(xn, Wkey, Wval, Wrec):
            k = jnp.einsum('bsd,fd->bsf', xn, Wkey)
            k = jnp.square(jax.nn.relu(k))
            v = jnp.einsum('bsf,df->bsd', k, Wval)
            r = jax.nn.sigmoid(jnp.einsum('bsd,ed->bse', xn, Wrec))
            return r * v

        def _reference_tuple_inner(x, ln1_g, ln1_b, ln2_g, ln2_b, Wr, Ww, Wk, Wv, Wo, time_decay, time_first, Wkey, Wval, Wrec):
            tm, new_state = _time_mix(_layernorm(x, ln1_g, ln1_b), Wr, Ww, Wk, Wv, Wo, time_decay)
            x = x + tm
            x = x + _channel_mix(_layernorm(x, ln2_g, ln2_b), Wkey, Wval, Wrec)
            return (x, new_state)
        return _reference_tuple_inner(x, ln1_g, ln1_b, ln2_g, ln2_b, Wr, Ww, Wk, Wv, Wo, time_decay, time_first, Wkey, Wval, Wrec)[0]

    def _L0_ffn_ref(x, expert_sel, keys, values):
        import jax, jax.numpy as jnp
        import numpy as np
        DMODEL = 256
        N_EXPERTS = 32
        EXPERT_SIZE = 128
        N_HEADS = 4
        WEIGHT_SCALE = 1.0
        B, S, D = x.shape
        xt = x.reshape(-1, D)
        N = xt.shape[0]
        sel_logits = jnp.einsum('nd,ed->ne', xt, expert_sel)
        gates = jax.nn.sigmoid(sel_logits)
        sel_val, sel_idx = jax.lax.top_k(gates, N_HEADS)
        gate_full = jnp.zeros_like(gates).at[jnp.arange(N)[:, None], sel_idx].set(sel_val)
        scores = jax.nn.relu(jnp.einsum('nd,edf->nef', xt, keys))
        scores = scores * gate_full[:, :, None]
        out = jnp.einsum('nef,efv->nv', scores, values)
        return out.reshape(B, S, -1)
    x = L0_attn_x
    x = x + _L0_attn_ref(_layernorm(x, axis=-1), L0_attn_ln1_g, L0_attn_ln1_b, L0_attn_ln2_g, L0_attn_ln2_b, L0_attn_Wr, L0_attn_Ww, L0_attn_Wk, L0_attn_Wv, L0_attn_Wo, L0_attn_time_decay, L0_attn_time_first, L0_attn_Wkey, L0_attn_Wval, L0_attn_Wrec)
    x = x + _L0_ffn_ref(_layernorm(x, axis=-1), L0_ffn_expert_sel, L0_ffn_keys, L0_ffn_values)
    return x

_drawn_inputs = setup_inputs


def setup_inputs(seed=0):
    import zlib

    import numpy as np

    out = dict(_drawn_inputs(seed))
    spreads = {'L0_attn_ln1_g': (1.0, 0.2),
     'L0_attn_ln1_b': (0.0, 0.1),
     'L0_attn_ln2_g': (1.0, 0.2),
     'L0_attn_ln2_b': (0.0, 0.288)}
    factors = {}
    for name, (base, spread) in spreads.items():
        noise = np.random.default_rng([zlib.crc32(name.encode()), seed]).standard_normal(out[name].shape)
        drawn = base * np.exp(spread * noise) if base else spread * noise
        out[name] = jnp.asarray(drawn.astype(out[name].dtype))
    for name, factor in factors.items():
        out[name] = (out[name] * factor).astype(out[name].dtype)
    return out
```

```python
from contextlib import ExitStack

import concourse.bass as bass
from concourse import mybir

F32 = mybir.dt.float32
F32R = mybir.dt.float32r
BF16 = mybir.dt.bfloat16
U32 = mybir.dt.uint32
I32 = mybir.dt.int32
ALU = mybir.AluOpType
ACT = mybir.ActivationFunctionType
AX_X = mybir.AxisListType.X

P = 128
LN_EPS = 1e-5
WKV_EPS = 1e-8

B, S, D, F = 8, 1024, 256, 1024
E, DE, TOPK = 32, 128, 4
N = B * S
TILE = 512
NT = N // TILE
J = TILE // P
KD = D // P
KF = F // P
assert S == 2 * TILE and D == 256

ROW = D + TOPK
BLOCK = 256
SUB = BLOCK // P
MAIN = N - TILE
LIST = MAIN + BLOCK
OVERFLOW = E * LIST
EMPTY = OVERFLOW + TOPK * TILE
LIST_ROWS = EMPTY + BLOCK
assert (TOPK + 1) * (MAIN + 1) > N * TOPK
RING = 8
NBLOCKS = -(-((N * TOPK - E) // BLOCK + E) // RING) * RING
OUT_ROWS = N * TOPK
SPACED = 2 * OUT_ROWS

C_IDENT, C_TRI, C_EXPERT, C_LIST, C_OUTROW, C_BLOCK = 0, 128, 256, 288, 320, 336
C_END = C_BLOCK + NBLOCKS


def after(eng, sem, count):
    if isinstance(count, int) and count <= 0:
        return
    eng.wait_ge(sem, count)


def program(nc, x, w_time, w_out, w_rec, w_key, w_val, ln_params, decay_in, sel_in, expert_in,
            consts_in, out, lists, expert_rows, residual):
    with ExitStack() as whole:
        def sem(name):
            return whole.enter_context(nc.semaphore(name))

        def keep(name, shape, dt=F32):
            return whole.enter_context(nc.sbuf_tensor(name, shape, dt))

        consts = keep("consts", [P, C_END])
        gates = keep("gates", [P, N // P, TOPK])
        list_end = keep("list_end", [P, E])
        count = keep("count", [P, E])
        full = keep("full", [P, E])
        zeros = keep("zeros", [P, SUB * ROW])
        ones_bf = keep("ones_bf", [P, P], BF16)
        tri_bf = keep("tri_bf", [P, P], BF16)
        ident = consts[:, C_IDENT:C_IDENT + P]

        consts_in_sbuf = sem("consts_in_sbuf")
        with ExitStack() as mix:
            mix_phase(nc, mix, sem, locals())
        with ExitStack() as experts:
            expert_phase(nc, experts, sem, locals())
        with ExitStack() as combine:
            combine_phase(nc, combine, sem, locals())


def mix_phase(nc, mix, sem, g):
    x, out = g["x"], g["out"]
    consts, gates, list_end, zeros = g["consts"], g["gates"], g["list_end"], g["zeros"]
    count, full = g["count"], g["full"]
    ones_bf, tri_bf, ident = g["ones_bf"], g["tri_bf"], g["ident"]
    residual, lists = g["residual"], g["lists"]

    def sb(name, shape, dt=F32):
        return mix.enter_context(nc.sbuf_tensor(name, shape, dt))

    wt_hi, wt_lo = (sb(f"wt_{h}", [P, 4, KD, D], F32R) for h in ("hi", "lo"))
    wo_hi, wo_lo = (sb(f"wo_{h}", [P, KD, D], F32R) for h in ("hi", "lo"))
    wr_hi, wr_lo = (sb(f"wr_{h}", [P, KD, D], F32R) for h in ("hi", "lo"))
    wk_hi, wk_lo = (sb(f"wk_{h}", [P, KD, F], F32R) for h in ("hi", "lo"))
    wv_hi, wv_lo = (sb(f"wv_{h}", [P, KF, D], F32R) for h in ("hi", "lo"))
    rec_bias_hi, rec_bias_lo = (sb(f"rec_bias_{h}", [1, D], F32R) for h in ("hi", "lo"))
    ones_row = sb("ones_row", [1, P], F32R)
    sel = sb("sel", [P, KD, E])
    decay = sb("decay", [P, KD])
    bias_t = sb("bias_t", [P, 8])
    bias_k = sb("bias_k", [P, KF])
    minus_half = sb("minus_half", [P, J])

    with ExitStack() as setup:
        def st(name, shape, dt=F32):
            return setup.enter_context(nc.sbuf_tensor(name, shape, dt))

        raw_t = st("raw_t", [P, 4, KD, D])
        raw_k = st("raw_k", [P, KD, F])
        raw_v = st("raw_v", [P, KF, D])
        raw_o = st("raw_o", [P, KD, D])
        raw_r = st("raw_r", [P, KD, D])
        rec_bias = st("rec_bias", [1, D])
        ones_f = st("ones_f", [P, P])
        time_decay = st("time_decay", [P, KD])
        ln = st("ln", [P, 4, KD])
        ps_b = setup.enter_context(nc.psum_tensor("ps_b", [P, 2, 512], F32))

        loaded = [sem(f"loaded_{n}") for n in ("consts", "t", "k", "v", "o", "r")]
        small_loaded = sem("small_loaded")
        bias_done = sem("bias_done")
        folded = sem("folded")
        split_hi = sem("split_hi")
        setup_v = sem("setup_v")

        with nc.Block() as block:
            @block.sync
            def _(sp):
                sp.dma_start(ln[:], g["ln_params"]).then_inc(small_loaded, 16)
                sp.dma_start(sel[:], g["sel_in"]).then_inc(small_loaded, 16)
                sp.dma_start(time_decay[:], g["decay_in"]).then_inc(small_loaded, 16)
                sp.dma_start(raw_t[:], g["w_time"]).then_inc(loaded[1], 16)
                sp.dma_start(raw_k[:], g["w_key"]).then_inc(loaded[2], 16)
                sp.dma_start(raw_r[:], g["w_rec"]).then_inc(loaded[5], 16)
                sp.dma_start(raw_o[:], g["w_out"]).then_inc(loaded[4], 16)
                sp.dma_start(raw_v[:], g["w_val"]).then_inc(loaded[3], 16)
                sp.dma_start(consts[:], g["consts_in"]).then_inc(loaded[0], 16)

            @block.tensor
            def _(pe):
                pe.wait_ge(small_loaded, 48)
                pe.wait_ge(loaded[1], 16)
                for m in range(8):
                    for k in range(KD):
                        pe.matmul(ps_b[:, 0, m:m + 1], raw_t[:, m // 2, k, (m % 2) * P:(m % 2 + 1) * P],
                                  ln[:, 1, k:k + 1], start=k == 0, stop=k == KD - 1)
                pe.wait_ge(loaded[2], 16)
                for m in range(KF):
                    for k in range(KD):
                        pe.matmul(ps_b[:, 0, 8 + m:9 + m], raw_k[:, k, m * P:(m + 1) * P],
                                  ln[:, 3, k:k + 1], start=k == 0, stop=k == KD - 1)
                pe.wait_ge(loaded[5], 16)
                for k in range(KD):
                    mm = pe.matmul(ps_b[0:1, 1, 0:D], ln[:, 3, k:k + 1], raw_r[:, k, :],
                                   start=k == 0, stop=k == KD - 1)
                mm.then_inc(bias_done, 1)

            @block.vector
            def _(dve):
                dve.memset(zeros[:], 0.0)
                dve.memset(ones_f[:], 1.0)
                dve.memset(minus_half[:], -0.5).then_inc(setup_v, 1)
                dve.wait_ge(setup_v, 1)
                dve.tensor_copy(ones_bf[:], ones_f[:])
                dve.tensor_copy(ones_row[:], ones_f[0:1, :])
                dve.wait_ge(loaded[0], 16)
                dve.tensor_copy(tri_bf[:], consts[:, C_TRI:C_TRI + P])
                dve.tensor_copy(list_end[:], consts[:, C_LIST:C_LIST + E])
                dve.wait_ge(bias_done, 1)
                dve.tensor_copy(bias_k[:], ps_b[:, 0, 8:16])
                dve.tensor_copy(rec_bias[:], ps_b[0:1, 1, 0:D])
                dve.tensor_copy(bias_t[:], ps_b[:, 0, 0:8]).then_inc(setup_v, 1)
                dve.wait_ge(setup_v, 2)
                dve.tensor_scalar(bias_t[:, 2:4], bias_t[:, 2:4], 0.5, None, ALU.mult)
                dve.tensor_copy(rec_bias_hi[:], rec_bias[:]).then_inc(setup_v, 1)
                dve.wait_ge(setup_v, 3)
                dve.tensor_tensor(rec_bias_lo[:], rec_bias[:], rec_bias_hi[:].bitcast(F32), ALU.subtract)
                for raw, gain, width in ((raw_t, 0, D), (raw_k, 2, F), (raw_r, 2, D)):
                    for k in range(KD):
                        part = raw[:, :, k, :] if raw is raw_t else raw[:, k, :]
                        ins = dve.tensor_scalar(part, part, ln[:, gain, k:k + 1], None, ALU.mult)
                    ins.then_inc(folded, 1)
                dve.wait_ge(loaded[3], 16)
                dve.tensor_scalar(raw_v[:], raw_v[:], 0.5, None, ALU.mult).then_inc(folded, 1)
                for n, (hi, lo, raw) in enumerate(((wt_hi, wt_lo, raw_t), (wk_hi, wk_lo, raw_k),
                                                   (wr_hi, wr_lo, raw_r), (wo_hi, wo_lo, raw_o),
                                                   (wv_hi, wv_lo, raw_v))):
                    dve.wait_ge(split_hi, n + 1)
                    dve.tensor_tensor(lo[:], raw[:], hi[:].bitcast(F32), ALU.subtract)

            @block.scalar
            def _(act):
                act.wait_ge(small_loaded, 48)
                act.activation(decay[:], time_decay[:], ACT.Exp)
                for n, (hi, raw) in enumerate(((wt_hi, raw_t), (wk_hi, raw_k), (wr_hi, raw_r),
                                               (wo_hi, raw_o), (wv_hi, raw_v))):
                    if raw is raw_o:
                        act.wait_ge(loaded[4], 16)
                    else:
                        act.wait_ge(folded, n + 1 if n < 3 else n)
                    act.activation(hi[:], raw[:], ACT.Copy).then_inc(split_hi, 1)

    x_sb = sb("x_sb", [P, 2, J, D])
    xn1 = sb("xn1", [P, 2, J, D])
    ratio = sb("ratio", [P, 2, J])
    xn1t_hi, xn1t_lo = (sb(f"xn1t_{h}", [P, KD, TILE], F32R) for h in ("hi", "lo"))
    th_r = sb("th_r", [P, KD, TILE])
    u = sb("u", [P, KD, TILE])
    den = sb("den", [P, KD, TILE])
    num = sb("num", [P, KD, TILE])
    carry = sb("carry", [P, 2, KD])
    y_hi, y_lo = (sb(f"y_{h}", [P, KD, TILE], F32R) for h in ("hi", "lo"))
    xp = sb("xp", [P, 2, J, D])
    xn2 = sb("xn2", [P, J, D])
    xn2t_hi, xn2t_lo = (sb(f"xn2t_{h}", [P, KD, TILE], F32R) for h in ("hi", "lo"))
    kr = sb("kr", [P, 2, TILE])
    ksq = sb("ksq", [P, 2, TILE])
    k_hi, k_lo = (sb(f"k_{h}", [P, KF, TILE], F32R) for h in ("hi", "lo"))
    th_c = sb("th_c", [P, J, D])
    rows = sb("rows", [P, 2, J, ROW])
    x3t = sb("x3t", [P, KD, TILE])
    stats = sb("stats", [P, 3, J, 6])
    mv = sb("mv", [P, 3, J, 2])
    rs = sb("rs", [P, 3, J])
    ln_a = sb("ln_a", [P, 3, J])
    ln_b = sb("ln_b", [P, J])
    ln_c = sb("ln_c", [P, J])
    ln_d = sb("ln_d", [P, J])
    eg = sb("eg", [P, J, E])
    gate = sb("gate", [P, J, E])
    top8 = sb("top8", [P, J, 8])
    top8_at = sb("top8_at", [P, J, 8], U32)
    chosen = sb("chosen", [P, J * TOPK, E])
    mask = sb("mask", [P, J, E], BF16)
    place = sb("place", [P, J, E])
    slot_f = sb("slot_f", [P, J * TOPK])
    slot = sb("slot", [P, 2, J * TOPK], U32)
    out_row = sb("out_row", [P, J, TOPK])
    expert = sb("expert", [P, J, TOPK])
    full_before = sb("full_before", [P, E])
    shift = sb("shift", [P, E])
    over = sb("over", [P, J, E])

    ps = mix.enter_context(nc.psum_tensor("ps", [P, 8, 512], F32))
    TR, PR, VAL, MISC = 0, 2, 4, 6

    def per(n):
        return [sem(s) for s in n.split()]

    x_loaded = per("x_loaded_even x_loaded_odd")
    x1_stored = per("x1_stored_even x1_stored_odd")
    scattered = per("scattered_even scattered_odd")
    t1_ready, proj_ready, o_ready, t2_ready, key_ready, t3_ready, logits_ready, rec_ready, val_ready, \
        rank_ready = per("t1_ready proj_ready o_ready t2_ready key_ready t3_ready logits_ready rec_ready "
                         "val_ready rank_ready")
    u_ready, thr_ready, e_ready, hi1_ready, yhi_ready, hi2_ready, kr_ready, ksq_ready, khi_ready, \
        x3t_ready, thc_ready, eg_ready = per("u_ready thr_ready e_ready hi1_ready yhi_ready hi2_ready "
                                             "kr_ready ksq_ready khi_ready x3t_ready thc_ready eg_ready")
    stats_ready = per("stats1_ready stats2_ready stats3_ready")
    mv_ready = per("mv1_ready mv2_ready mv3_ready")
    xn1_ready, xn1t_ready, ku_ready, ev_ready, den_ready, num_ready, carry_ready, rden_ready, thn_ready, \
        y_ready, xp_ready, xn2_ready, xn2t_ready, klo_ready, cm_ready, x1_ready, x3_ready = per(
            "xn1_ready xn1t_ready ku_ready ev_ready den_ready num_ready carry_ready rden_ready thn_ready "
            "y_ready xp_ready xn2_ready xn2t_ready klo_ready cm_ready x1_ready x3_ready")
    route_step, mask_ready, rank_used, place_ready, slot_ready = per(
        "route_step mask_ready rank_used place_ready slot_ready")
    rs_ready = per("rs1_ready rs2_ready rs3_ready")
    ln_step = per("ln1_step ln2_step ln3_step")
    over_done, area_cleared = per("over_done area_cleared")
    den2_ready, yprod_ready, xx_ready, placed_ready, scattered_q = per(
        "den2_ready yprod_ready xx_ready placed_ready scattered_q")

    def settled_on(eng, s, count):
        if isinstance(count, int):
            eng.wait_ge(s, count)
        else:
            with eng.register() as value:
                eng.reg_mov(value, count)
                eng.wait_ge(setup_v, 1)
                eng.wait_ge(s, value)

    def landed(eng, sems, p, pair, back, each=1):
        after(eng, sems[(p - back) % 2], 16 * each * (pair + (p - back) // 2 + 1))

    STEPS = NT + 3

    def stages(t):
        if not isinstance(t, int):
            return True, True, True, True, True
        return t < NT, 1 <= t <= NT, 2 <= t <= NT + 1, t + 1 < NT, 3 <= t <= NT + 2

    def run(eng, step):
        for t in range(4):
            step(t, t % 2, t // 2)
        with eng.Fori(2, NT // 2 - 1) as pair:
            step(2 * pair, 0, pair)
            step(2 * pair + 1, 1, pair)
        for t in range(NT - 2, STEPS):
            step(t, t % 2, t // 2)

    with nc.Block() as block:
        @block.sync
        def _(sp):
            sp.dma_start(x_sb[:, 0], x[0:TILE, :].rearrange("(j p) d -> p j d", p=P)).then_inc(x_loaded[0], 16)

            for row in range(OVERFLOW, LIST_ROWS, BLOCK):
                sp.dma_start(lists[row:row + BLOCK, :].rearrange("(p s) c -> p (s c)", p=P),
                             zeros[:]).then_inc(area_cleared, 16)

            def step(t, p, pair):
                has_t, has_u, has_v, has_next, _ = stages(t)
                if has_next:
                    after(sp, xx_ready, t)
                    sp.dma_start(x_sb[:, 1 - p], x[bass.ds((t + 1) * TILE, TILE), :]
                                 .rearrange("(j p) d -> p j d", p=P)).then_inc(x_loaded[1 - p], 16)
                if has_v:
                    after(sp, x1_ready, t - 1)
                    sp.dma_start(residual[bass.ds((t - 2) * TILE, TILE), :]
                                 .rearrange("(j p) d -> p j d", p=P), xp[:, p]).then_inc(x1_stored[p], 16)

            run(sp, step)
            for stored in x1_stored:
                sp.wait_ge(stored, 16 * NT // 2)

        @block.tensor
        def _(pe):
            def transposes(dst, src, k, ready):
                for j in range(J):
                    mm = pe.transpose(ps[:, dst + k, j * P:(j + 1) * P], src[:, j, k * P:(k + 1) * P], ident)
                mm.then_inc(ready, 1)

            def passes(bank, w_parts, x_parts, n_k, ready):
                (w_hi, w_lo), (x_hi, x_lo) = w_parts, x_parts
                last = 3 * n_k - 1
                n = 0
                for k in range(n_k):
                    for w, m in ((w_hi, x_hi), (w_hi, x_lo), (w_lo, x_hi)):
                        mm = pe.matmul(bank, w(k), m(k), start=n == 0, stop=n == last)
                        n += 1
                mm.then_inc(ready, 1)

            def t1(tile, q):
                after(pe, xn1_ready, tile + 1)
                after(pe, xn2t_ready, 2 * tile - 2)
                after(pe, rank_used, tile - 3)
                for k in range(KD):
                    transposes(TR, xn1[:, q], k, t1_ready)

            def step(t, p, pair):
                has_t, has_u, has_v, has_next, _ = stages(t)
                U, V = t - 1, t - 2
                if isinstance(t, int) and t == 0:
                    t1(t, 0)
                if has_t:
                    for m in range(8):
                        if m == 0:
                            after(pe, xn1t_ready, 2 * t + 2)
                            after(pe, eg_ready, t - 2)
                        elif m == 1:
                            after(pe, kr_ready, KF * (t - 1))
                        elif m in (2, 3):
                            pe.wait_ge(u_ready, 2 * t + m - 1)
                        elif m in (4, 5):
                            pe.wait_ge(thr_ready, 2 * t + m - 3)
                        else:
                            pe.wait_ge(ku_ready, 2 * t + m - 5)
                        c = slice((m % 2) * P, (m % 2 + 1) * P)
                        passes(ps[:, PR + m % 2, :],
                               (lambda k: wt_hi[:, m // 2, k, c], lambda k: wt_lo[:, m // 2, k, c]),
                               (lambda k: xn1t_hi[:, k, :], lambda k: xn1t_lo[:, k, :]), KD, proj_ready)
                if has_u:
                    after(pe, xn2_ready, U + 1)
                    after(pe, rank_used, V)
                    for k in range(KD):
                        transposes(TR, xn2, k, t2_ready)

                def key(m):
                    if m == 0:
                        pe.wait_ge(xn2t_ready, 2 * U + 2)
                    if m < 2:
                        if has_t:
                            pe.wait_ge(ev_ready, 2 * t + m + 1)
                        elif m == 0:
                            after(pe, eg_ready, V)
                        else:
                            after(pe, kr_ready, KF * U)
                    else:
                        pe.wait_ge(kr_ready, KF * U + m - 1)
                    passes(ps[:, PR + m % 2, :],
                           (lambda k: wk_hi[:, k, m * P:(m + 1) * P], lambda k: wk_lo[:, k, m * P:(m + 1) * P]),
                           (lambda k: xn2t_hi[:, k, :], lambda k: xn2t_lo[:, k, :]), KD, key_ready)

                if has_u:
                    for m in range(KF // 2):
                        key(m)
                if has_v:
                    after(pe, x3_ready, V + 1)
                    if has_u:
                        pe.wait_ge(xp_ready, U + 1)
                    for k in range(KD):
                        transposes(MISC, rows[:, p, :, 0:D], k, t3_ready)
                if has_u:
                    for m in range(KF // 2, KF):
                        key(m)
                if has_v:
                    pe.wait_ge(x3t_ready, 2 * V + 2)
                    if has_u:
                        pe.wait_ge(kr_ready, KF * U + KF - 1)
                    else:
                        pe.wait_ge(eg_ready, V)
                        pe.wait_ge(kr_ready, KF * NT)
                    for j in range(J):
                        for k in range(KD):
                            mm = pe.matmul(ps[:, PR, j * E:(j + 1) * E], x3t[:, k, j * P:(j + 1) * P],
                                           sel[:, k, :], start=k == 0, stop=k == KD - 1)
                    mm.then_inc(logits_ready, 1)
                if has_u:
                    if not has_v:
                        pe.wait_ge(xp_ready, U + 1)
                    for j in range(J):
                        bank = ps[:, MISC + j // 2, (j % 2) * D:(j % 2 + 1) * D]
                        pe.matmul(bank, ones_row[:], rec_bias_hi[:], start=True, stop=False)
                        pe.matmul(bank, ones_row[:], rec_bias_lo[:], start=False, stop=False)
                        c = slice(j * P, (j + 1) * P)
                        for k in range(KD):
                            pe.matmul(bank, xn2t_hi[:, k, c], wr_hi[:, k, :], start=False, stop=False)
                            pe.matmul(bank, xn2t_hi[:, k, c], wr_lo[:, k, :], start=False, stop=False)
                            mm = pe.matmul(bank, xn2t_lo[:, k, c], wr_hi[:, k, :], start=False, stop=k == KD - 1)
                    mm.then_inc(rec_ready, 1)
                if has_next:
                    t1(t + 1, 1 - p)
                if has_u:
                    if has_v:
                        pe.wait_ge(cm_ready, V + 1)
                    for f in range(KF):
                        pe.wait_ge(klo_ready, KF * U + f + 1)
                        for j in range(J):
                            bank = ps[:, VAL + j // 2, (j % 2) * D:(j % 2 + 1) * D]
                            c = slice(j * P, (j + 1) * P)
                            pe.matmul(bank, k_hi[:, f, c], wv_hi[:, f, :], start=f == 0 and j % 2 == 0,
                                      stop=False, skip_group_check=True)
                            pe.matmul(bank, k_hi[:, f, c], wv_lo[:, f, :], start=False, stop=False,
                                      skip_group_check=True)
                            mm = pe.matmul(bank, k_lo[:, f, c], wv_hi[:, f, :], start=False, stop=f == KF - 1,
                                           skip_group_check=True)
                    mm.then_inc(val_ready, 1)
                if has_v:
                    pe.wait_ge(mask_ready, V + 1)
                    if has_next:
                        pe.wait_ge(xn1t_ready, 2 * t + 4)
                    elif has_u:
                        pe.wait_ge(xn2t_ready, 2 * U + 2)
                    else:
                        pe.wait_ge(rank_used, V)
                    for j in range(J + 1):
                        cols = ps[:, TR, j * E:(j + 1) * E]
                        for i in range(j):
                            mm = pe.matmul(cols, ones_bf[:], mask[:, i, :], start=i == 0,
                                           stop=j == J and i == j - 1)
                        if j < J:
                            mm = pe.matmul(cols, tri_bf[:], mask[:, j, :], start=j == 0, stop=True)
                    mm.then_inc(rank_ready, 1)
                if has_t:
                    pe.wait_ge(y_ready, 2 * t + 2)
                    if has_u:
                        pe.wait_ge(thc_ready, U + 1)
                    for j in range(J):
                        bank = ps[:, MISC + j // 2, (j % 2) * D:(j % 2 + 1) * D]
                        c = slice(j * P, (j + 1) * P)
                        for k in range(KD):
                            pe.matmul(bank, y_hi[:, k, c], wo_hi[:, k, :], start=k == 0, stop=False)
                            pe.matmul(bank, y_hi[:, k, c], wo_lo[:, k, :], start=False, stop=False)
                            mm = pe.matmul(bank, y_lo[:, k, c], wo_hi[:, k, :], start=False, stop=k == KD - 1)
                    mm.then_inc(o_ready, 1)

            run(pe, step)

        @block.scalar
        def _(act):
            def hi1(tile):
                for k in range(KD):
                    act.wait_ge(t1_ready, 2 * tile + k + 1)
                    act.activation(xn1t_hi[:, k, :], ps[:, TR + k, :], ACT.Copy).then_inc(hi1_ready, 1)

            def step(t, p, pair):
                has_t, has_u, has_v, has_next, _ = stages(t)
                U, V = t - 1, t - 2
                if isinstance(t, int) and t == 0:
                    hi1(t)
                if has_t:
                    for m in range(KD):
                        act.wait_ge(proj_ready, 8 * t + m + 1)
                        act.activation(u[:, m, :], ps[:, PR + m, :], ACT.Exp,
                                       bias=bias_t[:, m:m + 1]).then_inc(u_ready, 1)
                    for m in range(KD):
                        act.wait_ge(proj_ready, 8 * t + m + 3)
                        act.activation(th_r[:, m, :], ps[:, PR + m, :], ACT.Tanh, scale=0.5,
                                       bias=bias_t[:, 2 + m:3 + m]).then_inc(thr_ready, 1)
                    for m in range(KD):
                        act.wait_ge(ku_ready, 2 * t + m + 1)
                        act.activation(den[:, m, :], u[:, m, :], ACT.Exp,
                                       bias=bias_t[:, 4 + m:5 + m]).then_inc(e_ready, 1)
                if has_u:
                    for k in range(KD):
                        act.wait_ge(t2_ready, 2 * U + k + 1)
                        act.activation(xn2t_hi[:, k, :], ps[:, TR + k, :], ACT.Copy).then_inc(hi2_ready, 1)

                def square(m):
                    act.wait_ge(kr_ready, KF * U + m + 1)
                    after(act, klo_ready, KF * U + m - 1)
                    act.activation(ksq[:, m % 2, :], kr[:, m % 2, :], ACT.Square).then_inc(ksq_ready, 1)
                    act.activation(k_hi[:, m, :], kr[:, m % 2, :], ACT.Square).then_inc(khi_ready, 1)

                for m in range(KF + 1):
                    if has_u and m < KF:
                        act.wait_ge(key_ready, KF * U + m + 1)
                        if m >= 2:
                            act.wait_ge(khi_ready, KF * U + m - 1)
                        act.activation(kr[:, m % 2, :], ps[:, PR + m % 2, :], ACT.Relu,
                                       bias=bias_k[:, m:m + 1]).then_inc(kr_ready, 1)
                    if has_u and m > 0:
                        square(m - 1)
                    if has_v and m == 5:
                        for k in range(KD):
                            act.wait_ge(t3_ready, 2 * V + k + 1)
                            act.activation(x3t[:, k, :], ps[:, MISC + k, :], ACT.Copy).then_inc(x3t_ready, 1)
                if has_v:
                    act.wait_ge(logits_ready, V + 1)
                    after(act, mask_ready, V)
                    act.activation(eg[:], ps[:, PR, 0:J * E].rearrange("p (j e) -> p j e", j=J), ACT.Exp,
                                   scale=-1.0).then_inc(eg_ready, 1)
                if has_u:
                    act.wait_ge(rec_ready, U + 1)
                    if has_v:
                        act.wait_ge(x1_ready, V + 1)
                    for h in range(2):
                        ins = act.activation(th_c[:, 2 * h:2 * h + 2, :],
                                             ps[:, MISC + h, :].rearrange("p (j d) -> p j d", j=2),
                                             ACT.Tanh, scale=0.5)
                    ins.then_inc(thc_ready, 1)
                if has_next:
                    hi1(t + 1)
                if has_t:
                    for m in range(KD):
                        act.wait_ge(yprod_ready, 2 * t + m + 1)
                        act.activation(y_hi[:, m, :], th_r[:, m, :], ACT.Copy).then_inc(yhi_ready, 1)

            run(act, step)

        @block.vector
        def _(dve):
            def settled(s, n):
                settled_on(dve, s, n)

            def ln_stats(n, src, tile):
                for j in range(J):
                    ins = dve.bn_stats(stats[:, n, j, :], src[:, j, :])
                ins.then_inc(stats_ready[n], 1)

            def ln_aggr(n, tile):
                settled(stats_ready[n], tile + 1)
                for j in range(J):
                    ins = dve.bn_aggr(mv[:, n, j, :], stats[:, n, j, :])
                ins.then_inc(mv_ready[n], 1)

            def ln_apply(n, dst, src, tile, ready):
                dve.wait_ge(rs_ready[n], tile + 1)
                for j in range(J):
                    ins = dve.tensor_scalar(dst[:, j, :], src[:, j, :], mv[:, n, j, 0:1], rs[:, n, j:j + 1],
                                            ALU.subtract, ALU.mult)
                ins.then_inc(ready, 1)

            def lo1(tile):
                for k in range(KD):
                    dve.wait_ge(hi1_ready, 2 * tile + k + 1)
                    dve.tensor_tensor(xn1t_lo[:, k, :], ps[:, TR + k, :], xn1t_hi[:, k, :].bitcast(F32),
                                      ALU.subtract).then_inc(xn1t_ready, 1)

            def first_norm_stats(tile, q):
                ln_stats(0, x_sb[:, q], tile)
                ln_aggr(0, tile)

            def step(t, p, pair):
                has_t, has_u, has_v, has_next, _ = stages(t)
                U, V = t - 1, t - 2
                if isinstance(t, int) and t == 0:
                    dve.tensor_copy(out_row[:], consts[:, C_OUTROW:C_OUTROW + J * TOPK]
                                    .rearrange("p (j k) -> p j k", j=J))
                    dve.wait_ge(x_loaded[0], 16)
                    first_norm_stats(t, 0)
                    ln_apply(0, xn1[:, 0], x_sb[:, 0], t, xn1_ready)
                    lo1(t)
                if has_u:
                    dve.wait_ge(o_ready, U + 1)
                    landed(dve, x1_stored, p, pair, 3)
                    for j in range(J):
                        ins = dve.scalar_tensor_tensor(
                            xp[:, 1 - p, j, :], xn1[:, 1 - p, j, :], ratio[:, 1 - p, j:j + 1],
                            ps[:, MISC + j // 2, (j % 2) * D:(j % 2 + 1) * D], ALU.mult, ALU.add)
                    ins.then_inc(xp_ready, 1)
                    dve.wait_ge(xp_ready, U + 1)
                    ln_stats(1, xp[:, 1 - p], U)
                    ln_aggr(1, U)
                if has_v:
                    dve.wait_ge(thc_ready, V + 1)
                    dve.wait_ge(val_ready, V + 1)
                    for h in range(2):
                        part = th_c[:, 2 * h:2 * h + 2, :].rearrange("p j d -> p (j d)")
                        ins = dve.scalar_tensor_tensor(part, part, 1.0, ps[:, VAL + h, :], ALU.add, ALU.mult)
                    ins.then_inc(cm_ready, 1)
                    dve.wait_ge(xx_ready, V + 1)
                    dve.wait_ge(cm_ready, V + 1)
                    dve.tensor_tensor(xp[:, p], xp[:, p], th_c[:], ALU.add).then_inc(x1_ready, 1)
                if has_u:
                    ln_apply(1, xn2, xp[:, 1 - p], U, xn2_ready)
                if has_t:
                    for m in range(KD):
                        dve.wait_ge(u_ready, 2 * t + m + 1)
                        dve.wait_ge(proj_ready, 8 * t + m + 5)
                        dve.tensor_tensor(u[:, m, :], ps[:, PR + m, :], u[:, m, :],
                                          ALU.subtract).then_inc(ku_ready, 1)
                if has_v:
                    dve.wait_ge(x1_ready, V + 1)
                    ln_stats(2, xp[:, p], V)
                if has_t:
                    for m in range(KD):
                        dve.wait_ge(e_ready, 2 * t + m + 1)
                        dve.wait_ge(proj_ready, 8 * t + m + 7)
                        dve.scalar_tensor_tensor(num[:, m, :], ps[:, PR + m, :], bias_t[:, 6 + m:7 + m],
                                                 den[:, m, :], ALU.add, ALU.mult).then_inc(ev_ready, 1)
                if has_v:
                    ln_aggr(2, V)
                if has_u:
                    for k in range(KD):
                        dve.wait_ge(hi2_ready, 2 * U + k + 1)
                        dve.tensor_tensor(xn2t_lo[:, k, :], ps[:, TR + k, :], xn2t_hi[:, k, :].bitcast(F32),
                                          ALU.subtract).then_inc(xn2t_ready, 1)
                if has_v:
                    landed(dve, scattered, p, pair, 4, J * TOPK)
                    ln_apply(2, rows[:, p, :, 0:D], xp[:, p], V, x3_ready)

                def k_rest(m):
                    if has_u:
                        dve.wait_ge(ksq_ready, KF * U + m + 1)
                        dve.wait_ge(khi_ready, KF * U + m + 1)
                        dve.tensor_tensor(k_lo[:, m, :], ksq[:, m % 2, :], k_hi[:, m, :].bitcast(F32),
                                          ALU.subtract).then_inc(klo_ready, 1)

                def scan(which, buf, m, before, ready):
                    if not has_t:
                        return
                    dve.wait_ge(before, 2 * t + m + 1)
                    if p == 1:
                        dve.wait_ge(carry_ready, t + 1)
                    dve.tensor_tensor_scan(buf[:, m, :], decay[:, m:m + 1].broadcast_to([P, TILE]),
                                           buf[:, m, :], 0.0 if p == 0 else carry[:, which, m:m + 1],
                                           ALU.mult, ALU.add).then_inc(ready, 1)

                def save_carry(which, buf, ready):
                    if has_t and p == 0:
                        dve.wait_ge(ready, 2 * t + 2)
                        dve.tensor_copy(carry[:, which, :], buf[:, :, TILE - 1]).then_inc(carry_ready, 1)

                k_rest(0)
                scan(0, den, 0, ev_ready, den_ready)
                k_rest(1)
                scan(0, den, 1, ev_ready, den_ready)
                k_rest(2)
                if has_next:
                    landed(dve, x_loaded, p, pair, -1)
                    first_norm_stats(t + 1, 1 - p)
                scan(1, num, 0, ev_ready, num_ready)
                k_rest(3)
                scan(1, num, 1, ev_ready, num_ready)
                k_rest(4)
                save_carry(0, den, den_ready)
                save_carry(1, num, num_ready)
                if has_next:
                    ln_apply(0, xn1[:, 1 - p], x_sb[:, 1 - p], t + 1, xn1_ready)
                k_rest(5)
                if has_t:
                    dve.wait_ge(den2_ready, 2 * t + 1)
                    dve.reciprocal(u[:, 0, :], u[:, 0, :]).then_inc(rden_ready, 1)
                k_rest(6)
                if has_t:
                    dve.wait_ge(num_ready, 2 * t + 2)
                    for m in range(KD):
                        dve.scalar_tensor_tensor(th_r[:, m, :], th_r[:, m, :], 1.0, num[:, m, :],
                                                 ALU.add, ALU.mult).then_inc(thn_ready, 1)
                k_rest(7)
                if has_t:
                    dve.wait_ge(den2_ready, 2 * t + 2)
                    dve.reciprocal(u[:, 1, :], u[:, 1, :]).then_inc(rden_ready, 1)
                if has_next:
                    lo1(t + 1)
                if has_v:
                    route(t, p, pair, V)
                if has_t:
                    for m in range(KD):
                        dve.wait_ge(yhi_ready, 2 * t + m + 1)
                        dve.tensor_tensor(y_lo[:, m, :], th_r[:, m, :], y_hi[:, m, :].bitcast(F32),
                                          ALU.subtract).then_inc(y_ready, 1)
                if has_v:
                    route_slots(t, p, pair, V)

            RS = 7

            def route(t, p, pair, V):
                def after_route(n):
                    dve.wait_ge(route_step, RS * V + n)

                dve.wait_ge(eg_ready, V + 1)
                dve.tensor_scalar(eg[:], eg[:], 1.0, None, ALU.add).then_inc(route_step, 1)
                after_route(1)
                dve.reciprocal(gate[:], eg[:]).then_inc(route_step, 1)
                settled(route_step, RS * V + 2)
                for j in range(J):
                    ins = dve.max(top8[:, j, :], gate[:, j, :])
                ins.then_inc(route_step, 1)
                settled(route_step, RS * V + 3)
                for j in range(J):
                    ins = dve.max_index(top8_at[:, j, :], top8[:, j, :], gate[:, j, :])
                ins.then_inc(route_step, 1)
                dve.tensor_copy(gates[:, bass.ds(V * J, J), :], top8[:, :, 0:TOPK])
                after_route(4)
                dve.tensor_copy(expert[:], top8_at[:, :, 0:TOPK]).then_inc(route_step, 1)
                after_route(5)
                dve.scalar_tensor_tensor(rows[:, p, :, D:ROW], expert[:], float(SPACED), out_row[:],
                                         ALU.mult, ALU.add).then_inc(route_step, 1)
                after_route(6)
                dve.tensor_scalar(out_row[:], out_row[:], float(TILE * TOPK), None, ALU.add)
                after(dve, placed_ready, V)
                dve.tensor_tensor(
                    chosen[:].rearrange("p (j k) e -> p j k e", j=J),
                    consts[:, C_EXPERT:C_EXPERT + E].unsqueeze(1).unsqueeze(1).broadcast_to([P, J, TOPK, E]),
                    expert[:].unsqueeze(3).broadcast_to([P, J, TOPK, E]),
                    ALU.is_equal).then_inc(route_step, 1)
                after_route(7)
                with nc.allow_low_precision(reason="counts of 0 and 1 are exact"):
                    dve.tensor_reduce(mask[:], chosen[:].rearrange("p (j k) e -> p j e k", j=J), AX_X,
                                      ALU.add).then_inc(mask_ready, 1)

            def route_slots(t, p, pair, V):
                dve.wait_ge(rank_ready, V + 1)
                dve.tensor_tensor(place[:], ps[:, TR, 0:J * E].rearrange("p (j e) -> p j e", j=J),
                                  list_end[:].unsqueeze(1).broadcast_to([P, J, E]),
                                  ALU.add).then_inc(place_ready, 1)
                dve.wait_ge(place_ready, V + 1)
                dve.tensor_tensor(list_end[:], ps[:, TR, J * E:(J + 1) * E], list_end[:],
                                  ALU.add).then_inc(rank_used, 1)
                if isinstance(t, int) and V == NT - 1:
                    overflow()
                dve.wait_ge(placed_ready, V + 1)
                dve.tensor_reduce(slot_f[:], chosen[:], AX_X, ALU.add).then_inc(place_summed, 1)
                dve.wait_ge(place_summed, V + 1)
                landed(dve, scattered, p, pair, 4, J * TOPK)
                dve.tensor_copy(slot[:, p, :], slot_f[:]).then_inc(slot_ready, 1)

            def overflow():
                n = [0]

                def chained(ins):
                    n[0] += 1
                    ins.then_inc(over_step, 1)
                    dve.wait_ge(over_step, n[0])

                first = consts[:, C_LIST:C_LIST + E]
                dve.wait_ge(rank_used, NT)
                chained(dve.tensor_tensor(count[:], list_end[:], first, ALU.subtract))
                chained(dve.tensor_scalar(full[:], count[:], float(MAIN), None, ALU.is_gt))
                chained(dve.tensor_tensor_scan(full_before[:], zeros[:, 0:E], full[:], 0.0, ALU.add, ALU.add))
                chained(dve.tensor_tensor(full_before[:], full_before[:], full[:], ALU.subtract))
                chained(dve.tensor_scalar(shift[:], full_before[:], float(TILE), float(OVERFLOW - MAIN),
                                          ALU.mult, ALU.add))
                chained(dve.tensor_tensor(shift[:], shift[:], first, ALU.subtract))
                dve.wait_ge(place_ready, NT)
                chained(dve.tensor_tensor(over[:], place[:], first.unsqueeze(1).broadcast_to([P, J, E]),
                                          ALU.subtract))
                chained(dve.tensor_scalar(over[:], over[:], float(MAIN), None, ALU.is_ge))
                chained(dve.tensor_tensor(over[:], over[:], shift[:].unsqueeze(1).broadcast_to([P, J, E]),
                                          ALU.mult))
                dve.tensor_tensor(place[:], place[:], over[:], ALU.add).then_inc(over_done, 1)

            over_step = sem("over_step")
            place_summed = sem("place_summed")
            run(dve, step)

        @block.gpsimd
        def _(pool):
            def ln_scale(n, tile):
                settled_on(pool, mv_ready[n], tile + 1)
                pool.tensor_scalar(ln_a[:, n, :], mv[:, n, :, 1], LN_EPS, 1.0, ALU.add,
                                   ALU.mult).then_inc(ln_step[n], 1)
                pool.wait_ge(ln_step[n], tile + 1)
                pool.tensor_tensor(rs[:, n, :], ln_a[:, n, :], minus_half[:], ALU.pow).then_inc(rs_ready[n], 1)

            L0 = 6

            def ln0_scale(tile, q):
                s = ln_step[0]
                settled_on(pool, mv_ready[0], tile + 1)
                pool.tensor_scalar(ln_a[:, 0, :], mv[:, 0, :, 1], LN_EPS, 1.0, ALU.add, ALU.mult).then_inc(s, 1)
                pool.wait_ge(s, L0 * tile + 1)
                pool.tensor_tensor(ln_b[:], ln_a[:, 0, :], minus_half[:], ALU.pow).then_inc(s, 1)
                pool.wait_ge(s, L0 * tile + 2)
                pool.tensor_tensor(ln_c[:], mv[:, 0, :, 1], ln_b[:], ALU.mult).then_inc(s, 1)
                pool.wait_ge(s, L0 * tile + 3)
                pool.tensor_tensor(ln_c[:], ln_c[:], ln_b[:], ALU.mult).then_inc(s, 1)
                settled_on(pool, s, L0 * tile + 4)
                pool.tensor_scalar(ln_a[:, 0, :], ln_c[:], LN_EPS, 1.0, ALU.add, ALU.mult).then_inc(s, 1)
                pool.wait_ge(s, L0 * tile + 5)
                pool.tensor_tensor(ln_d[:], ln_a[:, 0, :], minus_half[:], ALU.pow).then_inc(s, 1)
                pool.wait_ge(s, L0 * tile + 6)
                after(pool, xp_ready, tile - 1)
                pool.tensor_tensor(ratio[:, q, :], ln_a[:, 0, :], ln_d[:], ALU.mult)
                pool.tensor_tensor(rs[:, 0, :], ln_b[:], ln_d[:], ALU.mult).then_inc(rs_ready[0], 1)

            def scatter(t, q, part):
                W = t - 3
                if isinstance(W, int) and W == NT - 1:
                    pool.wait_ge(area_cleared, 16 * (LIST_ROWS - OVERFLOW) // BLOCK)
                if part == 0:
                    settled_on(pool, slot_ready, W + 1)
                j = part
                for k in range(TOPK):
                    pool.indirect_dma_start(
                        lists, bass.IndirectOffsetOnAxis(ap=slot[:, q, j * TOPK + k:j * TOPK + k + 1], axis=0),
                        rows[:, q, j, :], None).then_inc(scattered[q], 16)

            def step(t, p, pair):
                has_t, has_u, has_v, has_next, has_w = stages(t)
                U, V = t - 1, t - 2
                if isinstance(t, int) and t == 0:
                    ln0_scale(t, 0)
                if has_u:
                    ln_scale(1, U)
                    pool.wait_ge(xn2_ready, U + 1)
                    pool.tensor_tensor(xp[:, 1 - p], xp[:, 1 - p], x_sb[:, 1 - p], ALU.add).then_inc(xx_ready, 1)
                if has_w:
                    scatter(t, 1 - p, 0)
                if has_v:
                    ln_scale(2, V)
                if has_w:
                    scatter(t, 1 - p, 1)
                if has_t:
                    for m in range(KD):
                        settled_on(pool, den_ready, 2 * t + m + 1)
                        pool.tensor_scalar(u[:, m, :], den[:, m, :], WKV_EPS, 2.0, ALU.add,
                                           ALU.mult).then_inc(den2_ready, 1)
                if has_next:
                    ln0_scale(t + 1, 1 - p)
                if has_w:
                    scatter(t, 1 - p, 2)
                if has_t:
                    for m in range(KD):
                        pool.wait_ge(thn_ready, 2 * t + m + 1)
                        pool.wait_ge(rden_ready, 2 * t + m + 1)
                        pool.tensor_tensor(th_r[:, m, :], th_r[:, m, :], u[:, m, :],
                                           ALU.mult).then_inc(yprod_ready, 1)
                if has_w:
                    scatter(t, 1 - p, 3)
                if has_v:
                    pool.wait_ge(place_ready, V + 1)
                    if isinstance(t, int) and V == NT - 1:
                        pool.wait_ge(over_done, 1)
                    pool.tensor_tensor(chosen[:].rearrange("p (j k) e -> p j k e", j=J),
                                       chosen[:].rearrange("p (j k) e -> p j k e", j=J),
                                       place[:].unsqueeze(2).broadcast_to([P, J, TOPK, E]),
                                       ALU.mult).then_inc(placed_ready, 1)

            run(pool, step)
            for done in scattered:
                pool.wait_ge(done, 16 * NT // 2 * J * TOPK)


def expert_phase(nc, scope, sem, g):
    consts, zeros = g["consts"], g["zeros"]
    ones_bf, ident = g["ones_bf"], g["ident"]
    count, full = g["count"], g["full"]
    lists, expert_rows = g["lists"], g["expert_rows"]

    def sb(name, shape, dt=F32):
        return scope.enter_context(nc.sbuf_tensor(name, shape, dt))

    def sems(name, n):
        return [sem(f"{name}_{i}") for i in range(n)]

    W = KD * DE + D
    LOADS = 8
    w = sb("w", [P, E, 2, W], F32R)
    keys = sb("keys", [P, RING, 2, KD * DE], F32R)
    plan_expert = sb("plan_expert", [P, NBLOCKS], I32)
    plan_row = sb("plan_row", [P, NBLOCKS], I32)
    plan_mark = sb("plan_mark", [P, NBLOCKS])
    fill_row = sb("fill_row", [P, E], I32)
    blocks_i = sb("blocks_i", [P, E], I32)
    blocks = sb("blocks", [P, E])
    upto = sb("upto", [P, E])
    diag = sb("diag", [E, 3, E])
    column = sb("column", [E, 3])
    passed = sb("passed", [E, NBLOCKS], BF16)
    spread = sb("spread", [E, 2, P], BF16)
    pe_, pb, pf, pt, pr = (sb(f"plan_{n}", [P, NBLOCKS]) for n in "ebftr")
    xr = sb("xr", [P, RING, SUB, ROW])
    xt_hi, xt_lo = (sb(f"xt_{h}", [P, 2, KD, BLOCK], F32R) for h in ("hi", "lo"))
    h_hi, h_lo = (sb(f"h_{h}", [P, 2, BLOCK], F32R) for h in ("hi", "lo"))
    mark = sb("mark", [P, SUB, TOPK])
    dest = sb("dest", [P, RING, SUB], U32)
    y = sb("y", [P, RING, SUB, D])
    ps = scope.enter_context(nc.psum_tensor("ps2", [P, 8, 512], F32))
    XT, H, Y, PLAN = 0, 2, 4, 6

    filled, plan_step, plan_counts, plan_ready, whi_ready, w_ready = (
        sem(n) for n in "filled plan_step plan_counts plan_ready whi_ready w_ready".split())
    weights_loaded = sems("weights_loaded", LOADS)
    rows_loaded = sems("rows_loaded", RING)
    sent = sems("sent", RING)
    (xt_done, keys_ready, h_done, y_done, xhi_ready, x_ready, hhi_ready, h_ready, ycopy_ready, mark_ready,
     dest_ready) = (sem(n) for n in ("xt_done keys_ready h_done y_done xhi_ready x_ready hhi_ready "
                                     "h_ready ycopy_ready mark_ready dest_ready").split())

    def loop(eng, step, drain=0):
        for i in range(RING):
            step(i, i, 0)
        with eng.Fori(1, NBLOCKS // RING) as ring:
            for r in range(RING):
                step(RING * ring + r, r, ring)
        for i in range(NBLOCKS, NBLOCKS + drain):
            step(i, i % RING, i // RING)

    def settled_on(eng, s, n, also=None):
        if isinstance(n, int):
            eng.wait_ge(s, n)
            if also:
                eng.wait_ge(also, n)
        else:
            with eng.register() as value:
                eng.reg_mov(value, n)
                eng.wait_ge(plan_ready, 1)
                eng.wait_ge(s, value)
                if also:
                    eng.wait_ge(also, value)

    def part(n):
        return slice(n * (E // LOADS), (n + 1) * (E // LOADS))

    with nc.Block() as block:
        @block.sync
        def _(sp):
            for n in range(LOADS):
                sp.dma_start(w[:, part(n), 1, :].bitcast(F32), g["expert_in"][:, part(n), :]).then_inc(weights_loaded[n], 16)
            sp.wait_ge(plan_counts, 1)
            with sp.Fori(0, E) as e:
                row = sp.value_load(fill_row[0:1, bass.ds(e, 1)], min_val=0, max_val=OVERFLOW - BLOCK)
                sp.dma_start(lists[bass.ds(row, BLOCK), :].rearrange("(p s) c -> p (s c)", p=P),
                             zeros[:]).then_inc(filled, 16)
            sp.wait_ge(filled, 16 * E)
            sp.wait_ge(plan_ready, 1)

            def step(i, r, ring):
                after(sp, xt_done, i - RING + 1)
                after(sp, mark_ready, i - RING + 1)
                row = sp.value_load(plan_row[0:1, bass.ds(i, 1)], min_val=0, max_val=LIST_ROWS - BLOCK)
                sp.dma_start(xr[:, r], lists[bass.ds(row, BLOCK), :].rearrange("(p s) c -> p s c", p=P)
                             ).then_inc(rows_loaded[r], 16)

            loop(sp, step)

        @block.tensor
        def _(pe):
            pe.wait_ge(plan_counts, 2)
            for n, lhs in enumerate((ones_bf[0:E, :], spread[:, 0, :], spread[:, 1, :])):
                mm = pe.matmul(ps[:, PLAN + n // 2, (n % 2) * 256:(n % 2) * 256 + NBLOCKS], lhs, passed[:],
                               start=True, stop=True)
            mm.then_inc(plan_counts, 1)
            pe.wait_ge(plan_ready, 1)
            pe.wait_ge(w_ready, LOADS)

            def step(i, r, ring):
                if not isinstance(i, int) or i < NBLOCKS:
                    pe.wait_ge(rows_loaded[r], 16 * (ring + 1))
                    after(pe, x_ready, i - 1)
                    for k in range(KD):
                        for s in range(SUB):
                            mm = pe.transpose(ps[:, XT + r % 2, k * BLOCK + s * P:k * BLOCK + (s + 1) * P],
                                              xr[:, r, s, k * P:(k + 1) * P], ident)
                    mm.then_inc(xt_done, 1)
                if not isinstance(i, int) or i >= 2:
                    e = pe.value_load(plan_expert[0:1, bass.ds(i - 2, 1)], min_val=0, max_val=E - 1)
                q = (r - 1) % 2
                if not isinstance(i, int) or 1 <= i <= NBLOCKS:
                    pe.wait_ge(keys_ready, i)
                    pe.wait_ge(x_ready, i)
                    after(pe, h_ready, i - 2)
                    n = 0
                    for k in range(KD):
                        for part_, m in ((0, xt_hi), (0, xt_lo), (1, xt_hi)):
                            mm = pe.matmul(ps[:, H + q, 0:BLOCK],
                                           keys[:, (r - 1) % RING, part_, k * DE:(k + 1) * DE],
                                           m[:, q, k, :], start=n == 0, stop=n == 3 * KD - 1)
                            n += 1
                    mm.then_inc(h_done, 1)
                q = (r - 2) % 2
                if not isinstance(i, int) or i >= 2:
                    pe.wait_ge(h_ready, i - 1)
                    after(pe, ycopy_ready, i - 3)
                    v_hi, v_lo = (w[:, bass.ds(e, 1), h, KD * DE:].rearrange("p a w -> p (a w)") for h in (0, 1))
                    for s in range(SUB):
                        cols = ps[:, Y + q, s * D:(s + 1) * D]
                        c = slice(s * P, (s + 1) * P)
                        pe.matmul(cols, h_hi[:, q, c], v_hi, start=True, stop=False)
                        pe.matmul(cols, h_hi[:, q, c], v_lo, start=False, stop=False)
                        mm = pe.matmul(cols, h_lo[:, q, c], v_hi, start=False, stop=True)
                    mm.then_inc(y_done, 1)

            loop(pe, step, drain=2)

        @block.scalar
        def _(act):
            for n in range(LOADS):
                act.wait_ge(weights_loaded[n], 16)
                act.activation(w[:, part(n), 0, :], w[:, part(n), 1, :].bitcast(F32), ACT.Copy).then_inc(whi_ready, 1)

            def step(i, r, ring):
                q = r % 2
                if not isinstance(i, int) or i < NBLOCKS:
                    act.wait_ge(xt_done, i + 1)
                    after(act, h_done, i - 1)
                    act.activation(xt_hi[:, q].rearrange("p k b -> p (k b)"), ps[:, XT + q, :],
                                   ACT.Copy).then_inc(xhi_ready, 1)
                q = (r - 1) % 2
                if not isinstance(i, int) or 1 <= i <= NBLOCKS:
                    act.wait_ge(h_done, i)
                    after(act, y_done, i - 2)
                    act.activation(h_hi[:, q, :], ps[:, H + q, 0:BLOCK], ACT.Relu).then_inc(hhi_ready, 1)
                q = (r - 2) % 2
                if not isinstance(i, int) or i >= 2:
                    b = (r - 2) % RING
                    act.wait_ge(y_done, i - 1)
                    after(act, sent[b], 16 * SUB * (ring - 1 if r >= 2 else ring - 2) + 16 * SUB)
                    act.activation(y[:, b].rearrange("p s d -> p (s d)"), ps[:, Y + q, :],
                                   ACT.Copy).then_inc(ycopy_ready, 1)

            loop(act, step, drain=2)

        @block.vector
        def _(dve):
            n = [0]

            def chained(ins):
                n[0] += 1
                ins.then_inc(plan_step, 1)
                dve.wait_ge(plan_step, n[0])

            chained(dve.tensor_scalar(upto[:], count[:], float(MAIN), None, ALU.min))
            dve.tensor_tensor(fill_row[:], upto[:], consts[:, C_LIST:C_LIST + E], ALU.add).then_inc(plan_counts, 1)
            dve.wait_ge(plan_counts, 1)
            chained(dve.tensor_scalar(blocks_i[:], count[:], float(BLOCK - 1), None, ALU.add))
            chained(dve.tensor_scalar(blocks_i[:], blocks_i[:], BLOCK.bit_length() - 1, None,
                                      ALU.logical_shift_right))
            chained(dve.tensor_copy(blocks[:], blocks_i[:]))
            chained(dve.tensor_tensor_scan(upto[:], zeros[:, 0:E], blocks[:], 0.0, ALU.add, ALU.add))
            for c, row in enumerate((upto, blocks, full)):
                chained(dve.tensor_tensor(diag[:, c, :], row[0:E, :], ident[0:E, 0:E], ALU.mult))
            chained(dve.tensor_reduce(column[:], diag[:], AX_X, ALU.add))
            dve.tensor_scalar(passed[:], consts[0:E, C_BLOCK:C_END], column[:, 0:1], None, ALU.is_ge)
            dve.tensor_scalar(spread[:, 0, :], ones_bf[0:E, :], column[:, 1:2], None, ALU.mult)
            dve.tensor_scalar(spread[:, 1, :], ones_bf[0:E, :], column[:, 2:3], None,
                              ALU.mult).then_inc(plan_counts, 1)
            dve.wait_ge(plan_counts, 3)
            dve.tensor_copy(pe_[:], ps[:, PLAN, 0:NBLOCKS])
            dve.tensor_tensor(pb[:], consts[:, C_BLOCK:C_END], ps[:, PLAN, 256:256 + NBLOCKS], ALU.subtract)
            chained(dve.tensor_copy(pf[:], ps[:, PLAN + 1, 0:NBLOCKS]))
            chained(dve.tensor_scalar(plan_mark[:], pe_[:], 1.0, float(SPACED), ALU.add, ALU.mult))
            chained(dve.tensor_scalar(plan_expert[:], pe_[:], float(E - 1), None, ALU.min))
            chained(dve.tensor_scalar(pt[:], pe_[:], float(LIST), None, ALU.mult))
            chained(dve.scalar_tensor_tensor(pr[:], pb[:], float(BLOCK), pt[:], ALU.mult, ALU.add))
            chained(dve.scalar_tensor_tensor(pt[:], pf[:], float(TILE), pt[:], ALU.mult, ALU.subtract))
            chained(dve.tensor_scalar(pt[:], pt[:], float(OVERFLOW - MAIN), None, ALU.add))
            chained(dve.scalar_tensor_tensor(pt[:], pb[:], float(MAIN // BLOCK), pt[:], ALU.is_ge, ALU.mult))
            chained(dve.tensor_tensor(pr[:], pr[:], pt[:], ALU.add))
            chained(dve.tensor_scalar(pt[:], pr[:], -1.0, float(EMPTY), ALU.mult, ALU.add))
            chained(dve.scalar_tensor_tensor(pt[:], pe_[:], float(E), pt[:], ALU.is_ge, ALU.mult))
            dve.tensor_tensor(plan_row[:], pr[:], pt[:], ALU.add).then_inc(plan_ready, 1)
            for m in range(LOADS):
                dve.wait_ge(whi_ready, m + 1)
                dve.tensor_tensor(w[:, part(m), 1, :], w[:, part(m), 1, :].bitcast(F32),
                                  w[:, part(m), 0, :].bitcast(F32),
                                  ALU.subtract).then_inc(w_ready, 1)
            dve.wait_ge(plan_ready, 1)
            dve.wait_ge(w_ready, LOADS)

            expert = {}

            def load_expert(i, r):
                expert[r] = dve.value_load(plan_expert[0:1, bass.ds(i, 1)], min_val=0, max_val=E - 1)

            def step(i, r, ring):
                q, qh = r % 2, (r - 1) % 2
                a_block = not isinstance(i, int) or i < NBLOCKS
                if a_block:
                    if r == 0:
                        load_expert(i, r)
                    after(dve, h_done, i - RING + 1)
                    dve.tensor_copy(keys[:, r], w[:, bass.ds(expert[r], 1), :, 0:KD * DE].rearrange(
                        "p a h w -> p (a h) w").bitcast(F32)).then_inc(keys_ready, 1)
                    dve.wait_ge(rows_loaded[r], 16 * (ring + 1))
                    after(dve, dest_ready, i)
                    dve.tensor_scalar(mark[:], xr[:, r, :, D:ROW], plan_mark[:, bass.ds(i, 1)], None,
                                      ALU.subtract).then_inc(mark_ready, 1)
                    dve.wait_ge(xhi_ready, i + 1)
                    dve.tensor_tensor(xt_lo[:, q].rearrange("p k b -> p (k b)"), ps[:, XT + q, :],
                                      xt_hi[:, q].rearrange("p k b -> p (k b)").bitcast(F32),
                                      ALU.subtract).then_inc(x_ready, 1)
                    if r < RING - 1:
                        load_expert(i + 1, r + 1)
                if not isinstance(i, int) or 1 <= i <= NBLOCKS:
                    dve.wait_ge(hhi_ready, i)
                    dve.scalar_tensor_tensor(h_lo[:, qh, :], ps[:, H + qh, 0:BLOCK], 0.0,
                                             h_hi[:, qh, :].bitcast(F32), ALU.max, ALU.subtract
                                             ).then_inc(h_ready, 1)
                if a_block:
                    after(dve, sent[r], 16 * SUB * ring)
                    dve.wait_ge(mark_ready, i + 1)
                    dve.tensor_reduce(dest[:, r, :], mark[:], AX_X, ALU.min,
                                      apply_absolute_value=True).then_inc(dest_ready, 1)

            loop(dve, step, drain=1)

        @block.gpsimd
        def _(pool):
            def step(i, r, ring):
                settled_on(pool, ycopy_ready, i + 1, dest_ready)
                for s in range(SUB):
                    pool.indirect_dma_start(
                        expert_rows, bass.IndirectOffsetOnAxis(ap=dest[:, r, s:s + 1], axis=0), y[:, r, s, :],
                        None, bounds_check=OUT_ROWS - 1, oob_is_err=False).then_inc(sent[r], 16)

            loop(pool, step)
            for r in range(RING):
                pool.wait_ge(sent[r], 16 * SUB * NBLOCKS // RING)


def combine_phase(nc, scope, sem, g):
    gates, expert_rows, residual, out = g["gates"], g["expert_rows"], g["residual"], g["out"]
    GROUPS = 2
    STEPS = N // P // GROUPS
    DEPTH = 8
    ye = scope.enter_context(nc.sbuf_tensor("ye", [P, DEPTH, GROUPS, TOPK, D], F32))
    resid = scope.enter_context(nc.sbuf_tensor("resid", [P, DEPTH, GROUPS, D], F32))
    ye_loaded = [sem(f"ye_loaded_{r}") for r in range(DEPTH)]
    stored = [sem(f"stored_{r}") for r in range(DEPTH)]
    sum_step = sem("sum_step")

    with nc.Block() as block:
        def loop(eng, step):
            for i in range(DEPTH):
                step(i, i, 0)
            with eng.Fori(1, STEPS // DEPTH) as ring:
                for r in range(DEPTH):
                    step(DEPTH * ring + r, r, ring)

        @block.sync
        def _(sp):
            def step(i, r, ring):
                tokens = GROUPS * P
                after(sp, sum_step, TOPK * (i - DEPTH + 1))
                sp.dma_start(ye[:, r], expert_rows[bass.ds(i * (tokens * TOPK), tokens * TOPK), :]
                             .rearrange("(g p k) d -> p g k d", p=P, k=TOPK)).then_inc(ye_loaded[r], 16)
                after(sp, stored[r], 16 * ring)
                sp.dma_start(resid[:, r], residual[bass.ds(i * tokens, tokens), :]
                             .rearrange("(g p) d -> p g d", p=P)).then_inc(ye_loaded[r], 16)

            loop(sp, step)

        @block.vector
        def _(dve):
            def step(i, r, ring):
                dve.wait_ge(ye_loaded[r], 32 * (ring + 1))
                for k in range(TOPK):
                    after(dve, sum_step, TOPK * i + k)
                    for j in range(GROUPS):
                        ins = dve.scalar_tensor_tensor(
                            resid[:, r, j, :], ye[:, r, j, k, :],
                            gates[:, bass.ds(i * GROUPS + j, 1), k:k + 1].rearrange("p a b -> p (a b)"),
                            resid[:, r, j, :], ALU.mult, ALU.add)
                    ins.then_inc(sum_step, 1)

            loop(dve, step)

        @block.scalar
        def _(act):
            def step(i, r, ring):
                act.wait_ge(sum_step, TOPK * (i + 1))
                act.dma_start(out[bass.ds(i * (GROUPS * P), GROUPS * P), :].rearrange("(g p) d -> p g d", p=P),
                              resid[:, r]).then_inc(stored[r], 16)

            loop(act, step)
            for r in range(DEPTH):
                act.wait_ge(stored[r], 16 * STEPS // DEPTH)


def kernel(**inputs):
    import numpy as np
    import concourse.bacc as bacc
    from concourse.bass_utils import run_bass_kernel_spmd

    a = {n.removeprefix("L0_attn_").removeprefix("L0_ffn_"): np.asarray(v) for n, v in inputs.items()}

    def rows_first(w, k):
        return w.T.reshape(k, P, -1).transpose(1, 0, 2)

    consts = np.zeros((P, C_END), np.float32)
    p = np.arange(P)
    consts[:, C_IDENT:C_IDENT + P] = np.eye(P)
    consts[:, C_TRI:C_TRI + P] = p[:, None] < p[None, :]
    consts[:, C_EXPERT:C_EXPERT + E] = np.arange(E)
    consts[:, C_LIST:C_LIST + E] = np.arange(E) * LIST
    consts[:, C_OUTROW:C_OUTROW + J * TOPK] = ((np.arange(J)[None, :, None] * P + p[:, None, None]) * TOPK
                                              + np.arange(TOPK) + SPACED).reshape(P, -1)
    consts[:, C_BLOCK:C_END] = np.arange(NBLOCKS)
    laid = {
        "x": a["x"].reshape(N, D),
        "w_time": np.stack([rows_first(a[n], KD) for n in ("Ww", "Wr", "Wk", "Wv")], axis=1),
        "w_out": rows_first(a["Wo"], KD),
        "w_rec": rows_first(a["Wrec"], KD),
        "w_key": rows_first(a["Wkey"], KD),
        "w_val": rows_first(a["Wval"], KF),
        "ln_params": np.stack([a[n].reshape(KD, P).T for n in ("ln1_g", "ln1_b", "ln2_g", "ln2_b")], axis=1),
        "decay_in": a["time_decay"].reshape(KD, P).T,
        "sel_in": rows_first(a["expert_sel"], KD),
        "expert_in": np.concatenate([a["keys"].reshape(E, KD, P, DE).transpose(2, 0, 1, 3).reshape(P, E, KD * DE),
                                     a["values"].transpose(1, 0, 2)], axis=2),
        "consts_in": consts,
    }
    nc = bacc.Bacc("TRN2", target_bir_lowering=False, num_devices=1)
    arrays, args = {}, {}
    for name, v in laid.items():
        arrays[f"in_{name}"] = np.ascontiguousarray(v)
        args[name] = nc.dram_tensor(f"in_{name}", v.shape, mybir.dt.from_np(v.dtype), kind="ExternalInput").ap()
    args["out"] = nc.dram_tensor("out_dram", (N, D), F32, kind="ExternalOutput").ap()
    args["lists"] = nc.dram_tensor("lists", (LIST_ROWS, ROW), F32, kind="Internal").ap()
    args["expert_rows"] = nc.dram_tensor("expert_rows", (N * TOPK, D), F32, kind="Internal").ap()
    args["residual"] = nc.dram_tensor("residual", (N, D), F32, kind="Internal").ap()
    program(nc, **args)
    r = run_bass_kernel_spmd(nc, [arrays], core_ids=[0])
    return r.results[0]["out_dram"].reshape(B, S, D)
```

```python
from contextlib import ExitStack

import numpy as np

import concourse.bass as bass
from concourse import mybir

F32 = mybir.dt.float32
F32R = mybir.dt.float32r
BF16 = mybir.dt.bfloat16
U32 = mybir.dt.uint32
I32 = mybir.dt.int32
ALU = mybir.AluOpType
ACT = mybir.ActivationFunctionType
AX_X = mybir.AxisListType.X

P = 128
LN_EPS = 1e-5
WKV_EPS = 1e-8

B, S, D, F = 8, 1024, 256, 1024
E, DE, TOPK = 32, 128, 4
N = B * S
TILE = 512
NT = N // TILE
J = TILE // P
KD = D // P
KF = F // P
assert S == 2 * TILE and D == 256

ROW = D + TOPK
BLOCK = 256
SUB = BLOCK // P
MAIN = N - TILE
LIST = MAIN + BLOCK
OVERFLOW = E * LIST
EMPTY = OVERFLOW + TOPK * TILE
LIST_ROWS = EMPTY + BLOCK
assert (TOPK + 1) * (MAIN + 1) > N * TOPK
RING = 8
NBLOCKS = -(-((N * TOPK - E) // BLOCK + E) // RING) * RING
OUT_ROWS = N * TOPK
W = KD * DE + D
LOADS = 8
PART = E // LOADS
HEAD = 24
SPACED = 2 * OUT_ROWS

C_IDENT, C_TRI, C_EXPERT, C_LIST, C_OUTROW, C_BLOCK = 0, 128, 256, 288, 320, 336
C_END = C_BLOCK + NBLOCKS


def after(eng, sem, count):
    if isinstance(count, int) and count <= 0:
        return
    eng.wait_ge(sem, count)


def program(nc, x, w_time, w_out, w_rec, w_key, w_val, ln_params, decay_in, sel_in, expert_in,
            consts_in, out, lists, expert_rows, residual):
    with ExitStack() as whole:
        def sem(name):
            return whole.enter_context(nc.semaphore(name))

        def keep(name, shape, dt=F32):
            return whole.enter_context(nc.sbuf_tensor(name, shape, dt))

        consts = keep("consts", [P, C_END])
        gates = keep("gates", [P, N // P, TOPK])
        list_end = keep("list_end", [P, E])
        count = keep("count", [P, E])
        full = keep("full", [P, E])
        zeros = keep("zeros", [P, SUB * ROW])
        ones_bf = keep("ones_bf", [P, P], BF16)
        tri_bf = keep("tri_bf", [P, P], BF16)
        ident = consts[:, C_IDENT:C_IDENT + P]
        HALF = E * W * 4
        arena_at = -(-nc.sbuf_base // 32) * 32
        keep("arena", [P, 2, E * W])
        assert nc.sbuf_base == arena_at + 2 * HALF
        experts_w = nc.alloc_sbuf_tensor_at("experts_w", [P, 2, E, W], F32R, offset=arena_at)
        experts_raw = nc.alloc_sbuf_tensor_at("experts_raw", [P, E, W], F32, offset=arena_at + HALF)
        plan_expert = keep("plan_expert", [P, NBLOCKS], I32)
        plan_row = keep("plan_row", [P, NBLOCKS], I32)
        plan_mark = keep("plan_mark", [P, NBLOCKS])
        fill_row = keep("fill_row", [P, E], I32)
        plan_ready = sem("plan_ready")
        with ExitStack() as mix:
            mix_phase(nc, mix, sem, locals())
        resid_head = keep("resid_head", [P, HEAD, D])
        resid_head_loaded = sem("resid_head_loaded")
        with ExitStack() as experts:
            expert_phase(nc, experts, sem, locals())
        with ExitStack() as combine:
            combine_phase(nc, combine, sem, locals())


def mix_phase(nc, mix, sem, g):
    x, out = g["x"], g["out"]
    consts, gates, list_end, zeros = g["consts"], g["gates"], g["list_end"], g["zeros"]
    count, full = g["count"], g["full"]
    ones_bf, tri_bf, ident = g["ones_bf"], g["tri_bf"], g["ident"]
    residual, lists = g["residual"], g["lists"]
    experts_w, experts_raw, plan_ready = g["experts_w"], g["experts_raw"], g["plan_ready"]
    plan_expert, plan_row, plan_mark, fill_row = (g[n] for n in ("plan_expert", "plan_row", "plan_mark",
                                                                 "fill_row"))

    def sb(name, shape, dt=F32):
        return mix.enter_context(nc.sbuf_tensor(name, shape, dt))

    taken = [0, 0]

    def shared(half, name, shape, dt=F32R):
        start = taken[half]
        taken[half] += int(np.prod(shape)) * 4
        assert taken[half] <= g["HALF"]
        return nc.alloc_sbuf_tensor_at(name, [P] + shape, dt, offset=g["arena_at"] + half * g["HALF"] + start)

    def parts(half, name, shape):
        hi = shared(half, f"{name}_hi", shape)
        start = taken[half]
        lo = shared(half, f"{name}_lo", shape)
        raw = nc.alloc_sbuf_tensor_at(f"{name}_raw", [P] + shape, F32,
                                      offset=g["arena_at"] + half * g["HALF"] + start)
        return hi, lo, raw

    LO_ROW, BIAS_ROWS = 32, 64
    wt_hi, wt_lo, raw_t = parts(1, "wt", [4, KD, D])
    wo_hi, wo_lo, raw_o = parts(1, "wo", [KD, D])
    wk_hi, wk_lo, raw_k = parts(0, "wk", [KD, F])
    wv_hi, wv_lo, raw_v = parts(0, "wv", [KF, D])
    wr_hi, wr_lo = (sb(f"wr_{h}", [P, KD, D], F32R) for h in ("hi", "lo"))
    raw_r = nc.alloc_sbuf_tensor_at("wr_raw", [P, KD, D], F32, offset=g["arena_at"] + g["HALF"] - KD * D * 4)
    rec_bias = sb("rec_bias", [BIAS_ROWS, D], F32R)
    ones_rows = sb("ones_rows", [BIAS_ROWS, P], F32R)
    sel = sb("sel", [P, KD, E])
    decay = sb("decay", [P, KD])
    bias_t = sb("bias_t", [P, 8])
    bias_k = sb("bias_k", [P, KF])
    minus_half = sb("minus_half", [P, J])

    rec_bias_raw = sb("rec_bias_raw", [BIAS_ROWS, D])
    bias_columns = sb("bias_columns", [P, KD, BIAS_ROWS])
    ones_f = sb("ones_f", [P, P])
    ln = sb("ln", [P, 4, KD])

    loaded = {n: sem(f"loaded_{n}") for n in "consts t k v o r ln decay sel".split()}
    bias_done = sem("bias_done")
    folded = sem("folded")
    split_hi = sem("split_hi")
    split_lo = sem("split_lo")
    split_rest = sem("split_rest")
    setup_v = sem("setup_v")

    KRING = 4
    x_sb = sb("x_sb", [P, 2, J, D])
    xn1 = shared(1, "xn1", [2, J, D], F32)
    ratio = sb("ratio", [P, 2, J])
    xn1t_hi, xn1t_lo = (shared(1, f"xn1t_{h}", [KD, TILE]) for h in ("hi", "lo"))
    th_r = shared(1, "th_r", [KD, TILE], F32)
    u = shared(1, "u", [KD, TILE], F32)
    den = shared(1, "den", [KD, TILE], F32)
    num = shared(1, "num", [KD, TILE], F32)
    carry = sb("carry", [P, 2, KD])
    y_hi, y_lo = (shared(1, f"y_{h}", [KD, TILE]) for h in ("hi", "lo"))
    xp = sb("xp", [P, 2, J, D])
    xn2 = shared(1, "xn2", [J, D], F32)
    xn2t_hi, xn2t_lo = (sb(f"xn2t_{h}", [P, KD, TILE], F32R) for h in ("hi", "lo"))
    kr = sb("kr", [P, KRING, TILE])
    ksq = sb("ksq", [P, KRING, TILE])
    k_hi, k_lo = (shared(0, f"k_{h}", [KF, TILE]) for h in ("hi", "lo"))
    th_c = sb("th_c", [P, J, D])
    rows = sb("rows", [P, 2, J, ROW])
    x3t = sb("x3t", [P, KD, TILE])
    stats = sb("stats", [P, 3, J, 6])
    mv = sb("mv", [P, 3, J, 2])
    rs = sb("rs", [P, 3, J])
    shift_n = sb("shift_n", [P, 3, J])
    minus_mean = sb("minus_mean", [P, 3, J])
    ln_a = sb("ln_a", [P, 3, J])
    ln_b = sb("ln_b", [P, J])
    ln_c = sb("ln_c", [P, J])
    ln_d = sb("ln_d", [P, J])
    eg = sb("eg", [P, J, E])
    gate = sb("gate", [P, J, E])
    top8 = sb("top8", [P, J, 8])
    top8_at = sb("top8_at", [P, J, 8], U32)
    chosen = sb("chosen", [P, J * TOPK, E])
    mask = sb("mask", [P, J, E], BF16)
    place = sb("place", [P, J, E])
    slot_f = sb("slot_f", [P, J * TOPK])
    slot = sb("slot", [P, 2, J * TOPK], U32)
    out_row = sb("out_row", [P, J, TOPK])
    expert = sb("expert", [P, J, TOPK])
    full_before = sb("full_before", [P, E])
    shift = sb("shift", [P, E])
    over = sb("over", [P, J, E])
    blocks_i = sb("blocks_i", [P, E], I32)
    blocks = sb("blocks", [P, E])
    upto = sb("upto", [P, E])
    diag = sb("diag", [E, 3, E])
    column = sb("column", [E, 3])
    passed = sb("passed", [E, NBLOCKS], BF16)
    spread = sb("spread", [E, 2, P], BF16)
    pe_, pb, pf, pt = (kr[:, n, 0:NBLOCKS] for n in range(KRING))
    pr = kr[:, 0, TILE // 2:TILE // 2 + NBLOCKS]

    ps = mix.enter_context(nc.psum_tensor("ps", [P, 8, 512], F32))
    TR, PR, VAL, MISC = 0, 2, 4, 6
    PLAN = PR

    def per(n):
        return [sem(s) for s in n.split()]

    x_loaded = per("x_loaded_even x_loaded_odd")
    x1_stored = per("x1_stored_even x1_stored_odd")
    scattered = per("scattered_even scattered_odd")
    t1_ready, proj_ready, o_ready, t2_ready, key_ready, t3_ready, logits_ready, rec_ready, val_ready, \
        rank_ready = per("t1_ready proj_ready o_ready t2_ready key_ready t3_ready logits_ready rec_ready "
                         "val_ready rank_ready")
    u_ready, thr_ready, e_ready, hi1_ready, yhi_ready, hi2_ready, kr_ready, ksq_ready, khi_ready, \
        x3t_ready, thc_ready, eg_ready = per("u_ready thr_ready e_ready hi1_ready yhi_ready hi2_ready "
                                             "kr_ready ksq_ready khi_ready x3t_ready thc_ready eg_ready")
    stats_ready = per("stats1_ready stats2_ready stats3_ready")
    mv_ready = per("mv1_ready mv2_ready mv3_ready")
    xn2_last_ready, xn1_ready, xn1t_ready, ku_ready, ev_ready, den_ready, num_ready, carry_ready, rden_ready, \
        thn_ready, \
        y_ready, xp_ready, xn2_ready, xn2t_ready, klo_ready, cm_ready, x1_ready, x3_ready = per(
            "xn2_last_ready xn1_ready xn1t_ready ku_ready ev_ready den_ready num_ready carry_ready rden_ready "
            "thn_ready "
            "y_ready xp_ready xn2_ready xn2t_ready klo_ready cm_ready x1_ready x3_ready")
    route_step, mask_ready, rank_used, place_ready, slot_ready = per(
        "route_step mask_ready rank_used place_ready slot_ready")
    rs_ready = per("rs1_ready rs2_ready rs3_ready")
    ln_step = per("ln1_step ln2_step ln3_step")
    over_done, area_cleared = per("over_done area_cleared")
    plan_step, plan_counts, filled, experts_rounded, experts_split = per(
        "plan_step plan_counts filled experts_rounded experts_split")
    experts_loaded = [sem(f"experts_loaded_{n}") for n in range(LOADS)]
    den2_ready, yprod_ready, xx_ready, placed_ready, scattered_q = per(
        "den2_ready yprod_ready xx_ready placed_ready scattered_q")

    def settled_on(eng, s, count):
        if isinstance(count, int):
            eng.wait_ge(s, count)
        else:
            with eng.register() as value:
                eng.reg_mov(value, count)
                eng.wait_ge(setup_v, 1)
                eng.wait_ge(s, value)

    def landed(eng, sems, p, pair, back, each=1):
        after(eng, sems[(p - back) % 2], 16 * each * (pair + (p - back) // 2 + 1))

    STEPS = NT + 3

    def stages(t):
        if not isinstance(t, int):
            return True, True, True, True, True
        return t < NT, 1 <= t <= NT, 2 <= t <= NT + 1, t + 1 < NT, 3 <= t <= NT + 2

    def run(eng, step):
        for t in range(4):
            step(t, t % 2, t // 2)
        with eng.Fori(2, NT // 2 - 1) as pair:
            step(2 * pair, 0, pair)
            step(2 * pair + 1, 1, pair)
        for t in range(NT - 2, STEPS):
            step(t, t % 2, t // 2)

    def part(n):
        return slice(n * PART, (n + 1) * PART)

    def fill(eng, first, end):
        eng.wait_ge(plan_counts, 1)
        with eng.Fori(first, end) as e:
            row = eng.value_load(fill_row[0:1, bass.ds(e, 1)], min_val=0, max_val=OVERFLOW - BLOCK)
            eng.dma_start(lists[bass.ds(row, BLOCK), :].rearrange("(p s) c -> p (s c)", p=P),
                          zeros[:]).then_inc(filled, 16)
        eng.wait_ge(filled, 16 * E)

    with nc.Block() as block:
        @block.sync
        def _(sp):
            sp.dma_start(x_sb[:, 0], x[0:TILE, :].rearrange("(j p) d -> p j d", p=P)).then_inc(x_loaded[0], 16)
            for name, to, source in (("decay", decay[:], "decay_in"), ("ln", ln[:], "ln_params"),
                                     ("t", raw_t[:], "w_time"), ("consts", consts[:], "consts_in"),
                                     ("o", raw_o[:], "w_out"), ("k", raw_k[:], "w_key"),
                                     ("r", raw_r[:], "w_rec"), ("v", raw_v[:], "w_val"),
                                     ("sel", sel[:], "sel_in")):
                sp.dma_start(to, g[source]).then_inc(loaded[name], 16)
            sp.wait_ge(setup_v, 1)

            for row in range(OVERFLOW, LIST_ROWS, BLOCK):
                sp.dma_start(lists[row:row + BLOCK, :].rearrange("(p s) c -> p (s c)", p=P),
                             zeros[:]).then_inc(area_cleared, 16)

            def step(t, p, pair):
                has_t, has_u, has_v, has_next, _ = stages(t)
                if has_next:
                    after(sp, xx_ready, t)
                    sp.dma_start(x_sb[:, 1 - p], x[bass.ds((t + 1) * TILE, TILE), :]
                                 .rearrange("(j p) d -> p j d", p=P)).then_inc(x_loaded[1 - p], 16)
                if has_v:
                    after(sp, x1_ready, t - 1)
                    sp.dma_start(residual[bass.ds((t - 2) * TILE, TILE), :]
                                 .rearrange("(j p) d -> p j d", p=P), xp[:, p]).then_inc(x1_stored[p], 16)

                if isinstance(t, int) and t == NT:
                    sp.wait_ge(o_ready, NT)
                    sp.wait_ge(xp_ready, NT)
                    sp.wait_ge(t2_ready, 2 * NT)
                    for n in range(LOADS):
                        sp.dma_start(experts_raw[:, part(n), :], g["expert_in"][:, part(n), :]
                                     ).then_inc(experts_loaded[n], 16)

            run(sp, step)
            fill(sp, 0, E // 2)
            for stored in x1_stored:
                sp.wait_ge(stored, 16 * NT // 2)

        @block.tensor
        def _(pe):
            def transposes(dst, src, k, ready):
                for j in range(J):
                    mm = pe.transpose(ps[:, dst + k, j * P:(j + 1) * P], src[:, j, k * P:(k + 1) * P], ident)
                mm.then_inc(ready, 1)

            def passes(bank, w_parts, x_parts, n_k, ready):
                (w_hi, w_lo), (x_hi, x_lo) = w_parts, x_parts
                last = 3 * n_k - 1
                n = 0
                for k in range(n_k):
                    for w, m in ((w_hi, x_hi), (w_hi, x_lo), (w_lo, x_hi)):
                        mm = pe.matmul(bank, w(k), m(k), start=n == 0, stop=n == last)
                        n += 1
                mm.then_inc(ready, 1)

            def t1(tile, q):
                after(pe, xn1_ready, tile + 1)
                after(pe, xn2t_ready, 2 * tile - 2)
                after(pe, rank_used, tile - 3)
                for k in range(KD):
                    transposes(TR, xn1[:, q], k, t1_ready)

            def step(t, p, pair):
                has_t, has_u, has_v, has_next, _ = stages(t)
                U, V = t - 1, t - 2

                def second_transposes():
                    if has_u:
                        after(pe, xn2_ready, U + 1)
                        after(pe, xn2_last_ready, U + 1)
                        after(pe, rank_used, V)
                        for k in range(KD):
                            transposes(TR, xn2, k, t2_ready)

                if isinstance(t, int) and t == 0:
                    pe.wait_ge(loaded["ln"], 16)
                    pe.wait_ge(loaded["t"], 16)
                    for m in range(8):
                        for k in range(KD):
                            mm = pe.matmul(ps[:, MISC, m:m + 1], raw_t[:, m // 2, k, (m % 2) * P:(m % 2 + 1) * P],
                                           ln[:, 1, k:k + 1], start=k == 0, stop=k == KD - 1)
                    mm.then_inc(bias_done, 1)
                    pe.wait_ge(loaded["consts"], 16)
                    t1(t, 0)
                    pe.wait_ge(split_lo, 1)
                if has_t:
                    for m in range(8):
                        if m == 0:
                            after(pe, xn1t_ready, 2 * t + 2)
                            after(pe, eg_ready, t - 2)
                        elif m == 1:
                            after(pe, kr_ready, KF * (t - 1))
                        elif m in (2, 3):
                            pe.wait_ge(u_ready, 2 * t + m - 1)
                        elif m in (4, 5):
                            pe.wait_ge(thr_ready, 2 * t + m - 3)
                        elif m == 6:
                            second_transposes()
                            after(pe, cm_ready, t - 1)
                        c = slice((m % 2) * P, (m % 2 + 1) * P)
                        passes(ps[:, (PR if m < 6 else VAL) + m % 2, :],
                               (lambda k: wt_hi[:, m // 2, k, c], lambda k: wt_lo[:, m // 2, k, c]),
                               (lambda k: xn1t_hi[:, k, :], lambda k: xn1t_lo[:, k, :]), KD, proj_ready)
                elif has_u:
                    second_transposes()
                if isinstance(t, int) and t == 0:
                    pe.wait_ge(loaded["k"], 16)
                    for m in range(KF):
                        for k in range(KD):
                            pe.matmul(ps[:, MISC + 1, D + m:D + m + 1], raw_k[:, k, m * P:(m + 1) * P],
                                      ln[:, 3, k:k + 1], start=k == 0, stop=k == KD - 1)
                    pe.wait_ge(loaded["r"], 16)
                    for k in range(KD):
                        mm = pe.matmul(ps[0:BIAS_ROWS, MISC + 1, 0:D], bias_columns[:, k, :], raw_r[:, k, :],
                                       start=k == 0, stop=k == KD - 1)
                    mm.then_inc(bias_done, 1)

                def key(m):
                    if m == 0:
                        if isinstance(t, int) and U == 0:
                            pe.wait_ge(split_rest, 1)
                        pe.wait_ge(xn2t_ready, 2 * U + 2)
                    if m < 2:
                        if has_t:
                            pe.wait_ge(ku_ready, 2 * t + m + 1)
                        elif m == 0:
                            after(pe, eg_ready, V)
                        else:
                            after(pe, kr_ready, KF * U)
                    else:
                        pe.wait_ge(kr_ready, KF * U + m - 1)
                    passes(ps[:, PR + m % 2, :],
                           (lambda k: wk_hi[:, k, m * P:(m + 1) * P], lambda k: wk_lo[:, k, m * P:(m + 1) * P]),
                           (lambda k: xn2t_hi[:, k, :], lambda k: xn2t_lo[:, k, :]), KD, key_ready)

                if has_u:
                    for m in range(KF // 2):
                        key(m)
                if has_v:
                    after(pe, x3_ready, V + 1)
                    if has_u:
                        pe.wait_ge(xp_ready, U + 1)
                    for k in range(KD):
                        transposes(MISC, rows[:, p, :, 0:D], k, t3_ready)
                if has_u:
                    for m in range(KF // 2, KF):
                        key(m)
                if has_u:
                    if has_v:
                        pe.wait_ge(x3t_ready, 2 * V + 2)
                    else:
                        pe.wait_ge(xp_ready, U + 1)
                    if isinstance(t, int) and U == 0:
                        pe.wait_ge(split_rest, 2)
                    for j in range(J):
                        bank = ps[:, MISC + j // 2, (j % 2) * D:(j % 2 + 1) * D]
                        pe.matmul(bank, ones_rows[:], rec_bias[:], start=True, stop=False)
                        c = slice(j * P, (j + 1) * P)
                        for k in range(KD):
                            pe.matmul(bank, xn2t_hi[:, k, c], wr_hi[:, k, :], start=False, stop=False)
                            pe.matmul(bank, xn2t_hi[:, k, c], wr_lo[:, k, :], start=False, stop=False)
                            mm = pe.matmul(bank, xn2t_lo[:, k, c], wr_hi[:, k, :], start=False, stop=k == KD - 1)
                    mm.then_inc(rec_ready, 1)
                if has_v:
                    if not has_u:
                        pe.wait_ge(x3t_ready, 2 * V + 2)
                    if has_u:
                        pe.wait_ge(kr_ready, KF * U + KF - 1)
                        if isinstance(t, int) and V == 0:
                            pe.wait_ge(loaded["sel"], 16)
                    else:
                        pe.wait_ge(eg_ready, V)
                        pe.wait_ge(kr_ready, KF * NT)
                    for j in range(J):
                        for k in range(KD):
                            mm = pe.matmul(ps[:, PR, j * E:(j + 1) * E], x3t[:, k, j * P:(j + 1) * P],
                                           sel[:, k, :], start=k == 0, stop=k == KD - 1)
                    mm.then_inc(logits_ready, 1)
                if has_next:
                    t1(t + 1, 1 - p)
                if has_u:
                    if has_t:
                        pe.wait_ge(ev_ready, 2 * t + 2)
                    elif has_v:
                        pe.wait_ge(cm_ready, V + 1)
                    if isinstance(t, int) and U == 0:
                        pe.wait_ge(split_rest, 3)
                    for f in range(KF):
                        pe.wait_ge(klo_ready, KF * U + f + 1)
                        for j in range(J):
                            bank = ps[:, VAL + j // 2, (j % 2) * D:(j % 2 + 1) * D]
                            c = slice(j * P, (j + 1) * P)
                            pe.matmul(bank, k_hi[:, f, c], wv_hi[:, f, :], start=f == 0 and j % 2 == 0,
                                      stop=False, skip_group_check=True)
                            pe.matmul(bank, k_hi[:, f, c], wv_lo[:, f, :], start=False, stop=False,
                                      skip_group_check=True)
                            mm = pe.matmul(bank, k_lo[:, f, c], wv_hi[:, f, :], start=False, stop=f == KF - 1,
                                           skip_group_check=True)
                    mm.then_inc(val_ready, 1)
                if has_v:
                    pe.wait_ge(mask_ready, V + 1)
                    if has_next:
                        pe.wait_ge(xn1t_ready, 2 * t + 4)
                    elif has_u:
                        pe.wait_ge(xn2t_ready, 2 * U + 2)
                    else:
                        pe.wait_ge(rank_used, V)
                    for j in range(J + 1):
                        cols = ps[:, TR, j * E:(j + 1) * E]
                        for i in range(j):
                            mm = pe.matmul(cols, ones_bf[:], mask[:, i, :], start=i == 0,
                                           stop=j == J and i == j - 1)
                        if j < J:
                            mm = pe.matmul(cols, tri_bf[:], mask[:, j, :], start=j == 0, stop=True)
                    mm.then_inc(rank_ready, 1)
                if has_t:
                    if isinstance(t, int) and t == 0:
                        pe.wait_ge(split_lo, 2)
                    pe.wait_ge(y_ready, 2 * t + 2)
                    if has_u:
                        pe.wait_ge(thc_ready, U + 1)
                    for j in range(J):
                        bank = ps[:, MISC + j // 2, (j % 2) * D:(j % 2 + 1) * D]
                        c = slice(j * P, (j + 1) * P)
                        for k in range(KD):
                            pe.matmul(bank, y_hi[:, k, c], wo_hi[:, k, :], start=k == 0, stop=False)
                            pe.matmul(bank, y_hi[:, k, c], wo_lo[:, k, :], start=False, stop=False)
                            mm = pe.matmul(bank, y_lo[:, k, c], wo_hi[:, k, :], start=False, stop=k == KD - 1)
                    mm.then_inc(o_ready, 1)

            run(pe, step)
            pe.wait_ge(plan_counts, 2)
            for n, lhs in enumerate((ones_bf[0:E, :], spread[:, 0, :], spread[:, 1, :])):
                mm = pe.matmul(ps[:, PLAN + n // 2, (n % 2) * 256:(n % 2) * 256 + NBLOCKS], lhs, passed[:],
                               start=True, stop=True)
            mm.then_inc(plan_counts, 1)

        @block.scalar
        def _(act):
            def hi1(tile):
                for k in range(KD):
                    act.wait_ge(t1_ready, 2 * tile + k + 1)
                    act.activation(xn1t_hi[:, k, :], ps[:, TR + k, :], ACT.Copy).then_inc(hi1_ready, 1)

            def ln_apply(n, dst, src, tile, ready, subtiles=J):
                act.wait_ge(rs_ready[n], tile + 1)
                for j in range(subtiles):
                    ins = act.activation(dst[:, j, :], src[:, j, :], ACT.Identity, scale=rs[:, n, j:j + 1],
                                         bias=shift_n[:, n, j:j + 1])
                ins.then_inc(ready, 1)

            def step(t, p, pair):
                has_t, has_u, has_v, has_next, _ = stages(t)
                U, V = t - 1, t - 2
                last = isinstance(t, int) and V == NT - 1
                if isinstance(t, int) and t == 0:
                    act.wait_ge(loaded["decay"], 16)
                    act.activation(decay[:], decay[:], ACT.Exp)
                    act.wait_ge(loaded["ln"], 16)
                    act.wait_ge(loaded["t"], 16)
                    for k in range(KD):
                        ins = act.activation(wt_hi[:, :, k, :], raw_t[:, :, k, :], ACT.Identity,
                                             scale=ln[:, 0, k:k + 1])
                    ins.then_inc(split_hi, 1)
                    act.wait_ge(x_loaded[0], 16)
                    ln_apply(0, xn1[:, 0], x_sb[:, 0], t, xn1_ready)
                    hi1(t)
                    act.wait_ge(loaded["o"], 16)
                    act.activation(wo_hi[:], raw_o[:], ACT.Copy).then_inc(split_hi, 1)
                    act.wait_ge(setup_v, 4)
                if has_t:
                    for m in range(KD):
                        act.wait_ge(proj_ready, 8 * t + m + 1)
                        act.activation(u[:, m, :], ps[:, PR + m, :], ACT.Exp,
                                       bias=bias_t[:, m:m + 1]).then_inc(u_ready, 1)
                    for m in range(KD):
                        act.wait_ge(proj_ready, 8 * t + m + 3)
                        act.activation(th_r[:, m, :], ps[:, PR + m, :], ACT.Tanh, scale=0.5,
                                       bias=bias_t[:, 2 + m:3 + m]).then_inc(thr_ready, 1)
                if has_u:
                    ln_apply(1, xn2, xp[:, 1 - p], U, xn2_ready, J - 1)
                if has_t:
                    for m in range(KD):
                        act.wait_ge(ku_ready, 2 * t + m + 1)
                        act.activation(den[:, m, :], u[:, m, :], ACT.Exp,
                                       bias=bias_t[:, 4 + m:5 + m]).then_inc(e_ready, 1)
                if has_u:
                    for k in range(KD):
                        act.wait_ge(t2_ready, 2 * U + k + 1)
                        act.activation(xn2t_hi[:, k, :], ps[:, TR + k, :], ACT.Copy).then_inc(hi2_ready, 1)

                def relu(m):
                    if has_u:
                        act.wait_ge(key_ready, KF * U + m + 1)
                        if m >= KRING:
                            act.wait_ge(khi_ready, KF * U + m + 1 - KRING)
                        act.activation(kr[:, m % KRING, :], ps[:, PR + m % 2, :], ACT.Relu,
                                       bias=bias_k[:, m:m + 1]).then_inc(kr_ready, 1)

                def square(m):
                    if has_u:
                        act.wait_ge(kr_ready, KF * U + m + 1)
                        after(act, klo_ready, KF * U + m + 1 - KRING)
                        act.activation(ksq[:, m % KRING, :], kr[:, m % KRING, :], ACT.Square).then_inc(ksq_ready, 1)
                        act.activation(k_hi[:, m, :], kr[:, m % KRING, :], ACT.Square).then_inc(khi_ready, 1)

                relu(0)
                relu(1)
                square(0)
                if last:
                    round_experts(0, 5)
                relu(2)
                square(1)
                relu(3)
                square(2)
                relu(4)
                if has_v:
                    for k in range(KD):
                        act.wait_ge(t3_ready, 2 * V + k + 1)
                        act.activation(x3t[:, k, :], ps[:, MISC + k, :], ACT.Copy).then_inc(x3t_ready, 1)
                relu(5)
                relu(6)
                square(3)
                relu(7)
                square(4)
                if has_next:
                    after(act, xp_ready, t)
                    ln_apply(0, xn1[:, 1 - p], x_sb[:, 1 - p], t + 1, xn1_ready)
                square(5)
                square(6)
                square(7)
                if has_u:
                    act.wait_ge(rec_ready, U + 1)
                    if has_v:
                        act.wait_ge(x1_ready, V + 1)
                    for h in range(2):
                        ins = act.activation(th_c[:, 2 * h:2 * h + 2, :],
                                             ps[:, MISC + h, :].rearrange("p (j d) -> p j d", j=2),
                                             ACT.Tanh, scale=0.5)
                    ins.then_inc(thc_ready, 1)
                if has_v:
                    act.wait_ge(logits_ready, V + 1)
                    after(act, mask_ready, V)
                    act.activation(eg[:], ps[:, PR, 0:J * E].rearrange("p (j e) -> p j e", j=J), ACT.Exp,
                                   scale=-1.0).then_inc(eg_ready, 1)
                if has_next:
                    hi1(t + 1)
                if has_t:
                    for m in range(KD):
                        act.wait_ge(yprod_ready, 2 * t + m + 1)
                        act.activation(y_hi[:, m, :], th_r[:, m, :], ACT.Copy).then_inc(yhi_ready, 1)

                if isinstance(t, int) and t == 0:
                    for n, (hi, raw) in enumerate(((wk_hi, raw_k), (wr_hi, raw_r), (wv_hi, raw_v))):
                        act.wait_ge(folded, n + 1)
                        act.activation(hi[:], raw[:], ACT.Copy).then_inc(split_hi, 1)
                if last:
                    round_experts(5, LOADS)

            def round_experts(first, end):
                act.wait_ge(val_ready, NT)
                for n in range(first, end):
                    act.wait_ge(experts_loaded[n], 16)
                    act.activation(experts_w[:, 0, part(n), :], experts_raw[:, part(n), :],
                                   ACT.Copy).then_inc(experts_rounded, 1)

            run(act, step)
            fill(act, E // 2, E)

        @block.vector
        def _(dve):
            def settled(s, n):
                settled_on(dve, s, n)

            def ln_stats(n, src, tile):
                after(dve, rs_ready[n], tile)
                for j in range(J):
                    ins = dve.bn_stats(stats[:, n, j, :], src[:, j, :])
                ins.then_inc(stats_ready[n], 1)

            def ln_aggr(n, tile):
                settled(stats_ready[n], tile + 1)
                for j in range(J):
                    ins = dve.bn_aggr(mv[:, n, j, :], stats[:, n, j, :])
                ins.then_inc(mv_ready[n], 1)

            def lo1(tile):
                for k in range(KD):
                    dve.wait_ge(hi1_ready, 2 * tile + k + 1)
                    dve.tensor_tensor(xn1t_lo[:, k, :], ps[:, TR + k, :], xn1t_hi[:, k, :].bitcast(F32),
                                      ALU.subtract).then_inc(xn1t_ready, 1)

            def split(hi, lo, raw, n):
                dve.wait_ge(split_hi, n + 1)
                dve.tensor_tensor(lo[:], raw[:], hi[:].bitcast(F32),
                                  ALU.subtract).then_inc(split_lo, 1)

            def split_experts(first, end):
                for n in range(first, end):
                    dve.wait_ge(experts_rounded, n + 1)
                    dve.tensor_tensor(experts_w[:, 1, part(n), :], experts_raw[:, part(n), :],
                                      experts_w[:, 0, part(n), :].bitcast(F32),
                                      ALU.subtract).then_inc(experts_split, 1)

            def first_norm_stats(tile, q):
                ln_stats(0, x_sb[:, q], tile)
                ln_aggr(0, tile)

            def step(t, p, pair):
                has_t, has_u, has_v, has_next, _ = stages(t)
                U, V = t - 1, t - 2
                if isinstance(t, int) and t == 0:
                    dve.memset(minus_half[:], -0.5)
                    dve.memset(ones_f[:], 1.0)
                    dve.memset(zeros[:], 0.0).then_inc(setup_v, 1)
                    dve.wait_ge(x_loaded[0], 16)
                    first_norm_stats(t, 0)
                    dve.wait_ge(setup_v, 1)
                    dve.tensor_copy(ones_bf[:], ones_f[:])
                    dve.tensor_copy(ones_rows[:], ones_f[0:BIAS_ROWS, :])
                    dve.tensor_copy(bias_columns[:], zeros[:, 0:KD * BIAS_ROWS].rearrange("p (k h) -> p k h", k=KD)
                                    ).then_inc(setup_v, 1)
                    dve.wait_ge(bias_done, 1)
                    dve.wait_ge(loaded["ln"], 16)
                    dve.tensor_copy(bias_t[:], ps[:, MISC, 0:8]).then_inc(setup_v, 1)
                    dve.wait_ge(setup_v, 2)
                    for row in (0, LO_ROW):
                        dve.tensor_copy(bias_columns[:, :, row], ln[:, 3, :])
                    dve.wait_ge(setup_v, 3)
                    dve.tensor_scalar(bias_t[:, 2:4], bias_t[:, 2:4], 0.5, None, ALU.mult).then_inc(setup_v, 1)
                    dve.wait_ge(loaded["consts"], 16)
                    dve.tensor_copy(tri_bf[:], consts[:, C_TRI:C_TRI + P])
                    dve.tensor_copy(list_end[:], consts[:, C_LIST:C_LIST + E])
                    dve.tensor_copy(out_row[:], consts[:, C_OUTROW:C_OUTROW + J * TOPK]
                                    .rearrange("p (j k) -> p j k", j=J))
                    dve.wait_ge(split_hi, 1)
                    for k in range(KD):
                        ins = dve.scalar_tensor_tensor(wt_lo[:, :, k, :], raw_t[:, :, k, :], ln[:, 0, k:k + 1],
                                                       wt_hi[:, :, k, :].bitcast(F32), ALU.mult, ALU.subtract)
                    ins.then_inc(split_lo, 1)
                    lo1(t)
                    split(wo_hi, wo_lo, raw_o, 1)
                if has_u:
                    dve.wait_ge(o_ready, U + 1)
                    landed(dve, x1_stored, p, pair, 3)
                    for j in range(J):
                        ins = dve.scalar_tensor_tensor(
                            xp[:, 1 - p, j, :], xn1[:, 1 - p, j, :], ratio[:, 1 - p, j:j + 1],
                            ps[:, MISC + j // 2, (j % 2) * D:(j % 2 + 1) * D], ALU.mult, ALU.add)
                    ins.then_inc(xp_ready, 1)
                    dve.wait_ge(xp_ready, U + 1)
                    ln_stats(1, xp[:, 1 - p], U)
                    ln_aggr(1, U)
                if has_v:
                    dve.wait_ge(thc_ready, V + 1)
                    dve.wait_ge(val_ready, V + 1)
                    for h in range(2):
                        part = th_c[:, 2 * h:2 * h + 2, :].rearrange("p j d -> p (j d)")
                        ins = dve.scalar_tensor_tensor(part, part, 1.0, ps[:, VAL + h, :], ALU.add, ALU.mult)
                    ins.then_inc(cm_ready, 1)
                    dve.wait_ge(xx_ready, V + 1)
                    dve.wait_ge(cm_ready, V + 1)
                    dve.tensor_tensor(xp[:, p], xp[:, p], th_c[:], ALU.add).then_inc(x1_ready, 1)
                if has_u:
                    dve.wait_ge(rs_ready[1], U + 1)
                    dve.tensor_scalar(xn2[:, J - 1, :], xp[:, 1 - p, J - 1, :], mv[:, 1, J - 1, 0:1],
                                      rs[:, 1, J - 1:J], ALU.subtract, ALU.mult).then_inc(xn2_last_ready, 1)
                if has_t:
                    for m in range(KD):
                        dve.wait_ge(u_ready, 2 * t + m + 1)
                        dve.wait_ge(proj_ready, 8 * t + m + 5)
                        dve.tensor_tensor(u[:, m, :], ps[:, PR + m, :], u[:, m, :],
                                          ALU.subtract).then_inc(ku_ready, 1)
                if has_v:
                    dve.wait_ge(x1_ready, V + 1)
                    ln_stats(2, xp[:, p], V)
                if has_u:
                    for k in range(KD):
                        dve.wait_ge(hi2_ready, 2 * U + k + 1)
                        dve.tensor_tensor(xn2t_lo[:, k, :], ps[:, TR + k, :], xn2t_hi[:, k, :].bitcast(F32),
                                          ALU.subtract).then_inc(xn2t_ready, 1)
                if has_v:
                    ln_aggr(2, V)
                if has_t:
                    for m in range(KD):
                        dve.wait_ge(e_ready, 2 * t + m + 1)
                        dve.wait_ge(proj_ready, 8 * t + m + 7)
                        dve.scalar_tensor_tensor(num[:, m, :], ps[:, VAL + m, :], bias_t[:, 6 + m:7 + m],
                                                 den[:, m, :], ALU.add, ALU.mult).then_inc(ev_ready, 1)
                if has_v:
                    landed(dve, scattered, p, pair, 4, J * TOPK)
                    dve.wait_ge(rs_ready[2], V + 1)
                    for j in range(J):
                        ins = dve.tensor_scalar(rows[:, p, j, 0:D], xp[:, p, j, :], mv[:, 2, j, 0:1],
                                                rs[:, 2, j:j + 1], ALU.subtract, ALU.mult)
                    ins.then_inc(x3_ready, 1)
                if isinstance(t, int) and V == NT - 1:
                    split_experts(0, 4)

                def k_rest(m):
                    if has_u:
                        dve.wait_ge(ksq_ready, KF * U + m + 1)
                        dve.wait_ge(khi_ready, KF * U + m + 1)
                        dve.tensor_tensor(k_lo[:, m, :], ksq[:, m % KRING, :], k_hi[:, m, :].bitcast(F32),
                                          ALU.subtract).then_inc(klo_ready, 1)

                def scan(which, buf, m, before, ready):
                    if not has_t:
                        return
                    dve.wait_ge(before, 2 * t + m + 1)
                    if p == 1:
                        dve.wait_ge(carry_ready, t + 1)
                    dve.tensor_tensor_scan(buf[:, m, :], decay[:, m:m + 1].broadcast_to([P, TILE]),
                                           buf[:, m, :], 0.0 if p == 0 else carry[:, which, m:m + 1],
                                           ALU.mult, ALU.add).then_inc(ready, 1)

                def save_carry(which, buf, ready):
                    if has_t and p == 0:
                        dve.wait_ge(ready, 2 * t + 2)
                        dve.tensor_copy(carry[:, which, :], buf[:, :, TILE - 1]).then_inc(carry_ready, 1)

                scan(0, den, 0, ev_ready, den_ready)
                scan(0, den, 1, ev_ready, den_ready)
                scan(1, num, 0, ev_ready, num_ready)
                scan(1, num, 1, ev_ready, num_ready)
                if has_next:
                    landed(dve, x_loaded, p, pair, -1)
                    first_norm_stats(t + 1, 1 - p)
                save_carry(0, den, den_ready)
                save_carry(1, num, num_ready)
                if has_t:
                    dve.wait_ge(den2_ready, 2 * t + 1)
                    dve.reciprocal(u[:, 0, :], u[:, 0, :]).then_inc(rden_ready, 1)
                for m in range(4):
                    k_rest(m)
                if has_t:
                    dve.wait_ge(den2_ready, 2 * t + 2)
                    dve.reciprocal(u[:, 1, :], u[:, 1, :]).then_inc(rden_ready, 1)
                    dve.wait_ge(num_ready, 2 * t + 2)
                    for m in range(KD):
                        dve.scalar_tensor_tensor(th_r[:, m, :], th_r[:, m, :], 1.0, num[:, m, :],
                                                 ALU.add, ALU.mult).then_inc(thn_ready, 1)
                for m in range(4, KF):
                    k_rest(m)
                if isinstance(t, int) and t == 0:
                    dve.wait_ge(bias_done, 2)
                    dve.tensor_copy(bias_k[:], ps[:, MISC + 1, D:D + KF])
                    dve.tensor_copy(rec_bias_raw[:], ps[0:BIAS_ROWS, MISC + 1, 0:D]).then_inc(setup_v, 1)
                if has_next:
                    lo1(t + 1)
                if has_v:
                    route(t, p, pair, V)
                if has_t:
                    for m in range(KD):
                        dve.wait_ge(yhi_ready, 2 * t + m + 1)
                        dve.tensor_tensor(y_lo[:, m, :], th_r[:, m, :], y_hi[:, m, :].bitcast(F32),
                                          ALU.subtract).then_inc(y_ready, 1)
                if isinstance(t, int) and t == 0:
                    dve.wait_ge(setup_v, 5)
                    dve.tensor_copy(rec_bias[:], rec_bias_raw[:]).then_inc(setup_v, 1)
                    dve.wait_ge(setup_v, 6)
                    lo_rows = slice(LO_ROW, BIAS_ROWS)
                    dve.tensor_tensor(rec_bias[lo_rows, :], rec_bias_raw[lo_rows, :],
                                      rec_bias[lo_rows, :].bitcast(F32), ALU.subtract)
                    for raw in (raw_k, raw_r):
                        for k in range(KD):
                            ins = dve.tensor_scalar(raw[:, k, :], raw[:, k, :], ln[:, 2, k:k + 1], None, ALU.mult)
                        ins.then_inc(folded, 1)
                    dve.wait_ge(loaded["v"], 16)
                    dve.tensor_scalar(raw_v[:], raw_v[:], 0.5, None, ALU.mult).then_inc(folded, 1)
                if has_v:
                    route_slots(t, p, pair, V)

            RS = 7

            def route(t, p, pair, V):
                def after_route(n):
                    dve.wait_ge(route_step, RS * V + n)

                dve.wait_ge(eg_ready, V + 1)
                dve.tensor_scalar(eg[:], eg[:], 1.0, None, ALU.add).then_inc(route_step, 1)
                after_route(1)
                dve.reciprocal(gate[:], eg[:]).then_inc(route_step, 1)
                settled(route_step, RS * V + 2)
                for j in range(J):
                    ins = dve.max(top8[:, j, :], gate[:, j, :])
                ins.then_inc(route_step, 1)
                settled(route_step, RS * V + 3)
                for j in range(J):
                    ins = dve.max_index(top8_at[:, j, :], top8[:, j, :], gate[:, j, :])
                ins.then_inc(route_step, 1)
                dve.tensor_copy(gates[:, bass.ds(V * J, J), :], top8[:, :, 0:TOPK])
                after_route(4)
                dve.tensor_copy(expert[:], top8_at[:, :, 0:TOPK]).then_inc(route_step, 1)
                after_route(5)
                dve.scalar_tensor_tensor(rows[:, p, :, D:ROW], expert[:], float(SPACED), out_row[:],
                                         ALU.mult, ALU.add).then_inc(route_step, 1)
                after_route(6)
                dve.tensor_scalar(out_row[:], out_row[:], float(TILE * TOPK), None, ALU.add)
                after(dve, placed_ready, V)
                dve.tensor_tensor(
                    chosen[:].rearrange("p (j k) e -> p j k e", j=J),
                    consts[:, C_EXPERT:C_EXPERT + E].unsqueeze(1).unsqueeze(1).broadcast_to([P, J, TOPK, E]),
                    expert[:].unsqueeze(3).broadcast_to([P, J, TOPK, E]),
                    ALU.is_equal).then_inc(route_step, 1)
                after_route(7)
                with nc.allow_low_precision(reason="counts of 0 and 1 are exact"):
                    dve.tensor_reduce(mask[:], chosen[:].rearrange("p (j k) e -> p j e k", j=J), AX_X,
                                      ALU.add).then_inc(mask_ready, 1)

            def route_slots(t, p, pair, V):
                dve.wait_ge(rank_ready, V + 1)
                dve.tensor_tensor(place[:], ps[:, TR, 0:J * E].rearrange("p (j e) -> p j e", j=J),
                                  list_end[:].unsqueeze(1).broadcast_to([P, J, E]),
                                  ALU.add).then_inc(place_ready, 1)
                dve.wait_ge(place_ready, V + 1)
                dve.tensor_tensor(list_end[:], ps[:, TR, J * E:(J + 1) * E], list_end[:],
                                  ALU.add).then_inc(rank_used, 1)
                if isinstance(t, int) and V == NT - 1:
                    overflow()
                dve.wait_ge(placed_ready, V + 1)
                dve.tensor_reduce(slot_f[:], chosen[:], AX_X, ALU.add).then_inc(place_summed, 1)
                dve.wait_ge(place_summed, V + 1)
                landed(dve, scattered, p, pair, 4, J * TOPK)
                dve.tensor_copy(slot[:, p, :], slot_f[:]).then_inc(slot_ready, 1)

            def overflow():
                n = [0]

                def chained(ins):
                    n[0] += 1
                    ins.then_inc(over_step, 1)
                    dve.wait_ge(over_step, n[0])

                first = consts[:, C_LIST:C_LIST + E]
                dve.wait_ge(rank_used, NT)
                chained(dve.tensor_tensor(count[:], list_end[:], first, ALU.subtract))
                chained(dve.tensor_scalar(upto[:], count[:], float(MAIN), None, ALU.min))
                dve.tensor_tensor(fill_row[:], upto[:], first, ALU.add).then_inc(plan_counts, 1)
                chained(dve.tensor_scalar(full[:], count[:], float(MAIN), None, ALU.is_gt))
                chained(dve.tensor_tensor_scan(full_before[:], zeros[:, 0:E], full[:], 0.0, ALU.add, ALU.add))
                chained(dve.tensor_tensor(full_before[:], full_before[:], full[:], ALU.subtract))
                chained(dve.tensor_scalar(shift[:], full_before[:], float(TILE), float(OVERFLOW - MAIN),
                                          ALU.mult, ALU.add))
                chained(dve.tensor_tensor(shift[:], shift[:], first, ALU.subtract))
                dve.wait_ge(place_ready, NT)
                chained(dve.tensor_tensor(over[:], place[:], first.unsqueeze(1).broadcast_to([P, J, E]),
                                          ALU.subtract))
                chained(dve.tensor_scalar(over[:], over[:], float(MAIN), None, ALU.is_ge))
                chained(dve.tensor_tensor(over[:], over[:], shift[:].unsqueeze(1).broadcast_to([P, J, E]),
                                          ALU.mult))
                dve.tensor_tensor(place[:], place[:], over[:], ALU.add).then_inc(over_done, 1)

            def make_plan():
                n = [0]

                def chained(ins):
                    n[0] += 1
                    ins.then_inc(plan_step, 1)
                    dve.wait_ge(plan_step, n[0])

                dve.wait_ge(plan_counts, 1)
                chained(dve.tensor_scalar(blocks_i[:], count[:], float(BLOCK - 1), None, ALU.add))
                chained(dve.tensor_scalar(blocks_i[:], blocks_i[:], BLOCK.bit_length() - 1, None,
                                          ALU.logical_shift_right))
                chained(dve.tensor_copy(blocks[:], blocks_i[:]))
                chained(dve.tensor_tensor_scan(upto[:], zeros[:, 0:E], blocks[:], 0.0, ALU.add, ALU.add))
                for c, row in enumerate((upto, blocks, full)):
                    chained(dve.tensor_tensor(diag[:, c, :], row[0:E, :], ident[0:E, 0:E], ALU.mult))
                chained(dve.tensor_reduce(column[:], diag[:], AX_X, ALU.add))
                dve.tensor_scalar(passed[:], consts[0:E, C_BLOCK:C_END], column[:, 0:1], None, ALU.is_ge)
                dve.tensor_scalar(spread[:, 0, :], ones_bf[0:E, :], column[:, 1:2], None, ALU.mult)
                dve.tensor_scalar(spread[:, 1, :], ones_bf[0:E, :], column[:, 2:3], None,
                                  ALU.mult).then_inc(plan_counts, 1)
                dve.wait_ge(plan_counts, 3)
                dve.tensor_copy(pe_[:], ps[:, PLAN, 0:NBLOCKS])
                dve.tensor_tensor(pb[:], consts[:, C_BLOCK:C_END], ps[:, PLAN, 256:256 + NBLOCKS], ALU.subtract)
                chained(dve.tensor_copy(pf[:], ps[:, PLAN + 1, 0:NBLOCKS]))
                chained(dve.tensor_scalar(plan_mark[:], pe_[:], 1.0, float(SPACED), ALU.add, ALU.mult))
                chained(dve.tensor_scalar(plan_expert[:], pe_[:], float(E - 1), None, ALU.min))
                chained(dve.tensor_scalar(pt[:], pe_[:], float(LIST), None, ALU.mult))
                chained(dve.scalar_tensor_tensor(pr[:], pb[:], float(BLOCK), pt[:], ALU.mult, ALU.add))
                chained(dve.scalar_tensor_tensor(pt[:], pf[:], float(TILE), pt[:], ALU.mult, ALU.subtract))
                chained(dve.tensor_scalar(pt[:], pt[:], float(OVERFLOW - MAIN), None, ALU.add))
                chained(dve.scalar_tensor_tensor(pt[:], pb[:], float(MAIN // BLOCK), pt[:], ALU.is_ge, ALU.mult))
                chained(dve.tensor_tensor(pr[:], pr[:], pt[:], ALU.add))
                chained(dve.tensor_scalar(pt[:], pr[:], -1.0, float(EMPTY), ALU.mult, ALU.add))
                chained(dve.scalar_tensor_tensor(pt[:], pe_[:], float(E), pt[:], ALU.is_ge, ALU.mult))
                dve.tensor_tensor(plan_row[:], pr[:], pt[:], ALU.add).then_inc(plan_ready, 1)

            over_step = sem("over_step")
            place_summed = sem("place_summed")
            run(dve, step)
            make_plan()
            split_experts(4, LOADS)

        @block.gpsimd
        def _(pool):
            def ln_scale(n, tile):
                settled_on(pool, mv_ready[n], tile + 1)
                pool.tensor_scalar(ln_a[:, n, :], mv[:, n, :, 1], LN_EPS, 1.0, ALU.add,
                                   ALU.mult).then_inc(ln_step[n], 1)
                pool.tensor_scalar(minus_mean[:, n, :], mv[:, n, :, 0], 0.0, -1.0, ALU.add, ALU.mult)
                pool.wait_ge(ln_step[n], LN * tile + 1)
                pool.tensor_tensor(rs[:, n, :], ln_a[:, n, :], minus_half[:], ALU.pow).then_inc(ln_step[n], 1)
                pool.wait_ge(ln_step[n], LN * tile + 2)
                pool.tensor_tensor(shift_n[:, n, :], minus_mean[:, n, :], rs[:, n, :],
                                   ALU.mult).then_inc(rs_ready[n], 1)

            LN = 2
            L0 = 7

            def ln0_scale(tile, q):
                s = ln_step[0]
                settled_on(pool, mv_ready[0], tile + 1)
                pool.tensor_scalar(ln_a[:, 0, :], mv[:, 0, :, 1], LN_EPS, 1.0, ALU.add, ALU.mult).then_inc(s, 1)
                pool.tensor_scalar(minus_mean[:, 0, :], mv[:, 0, :, 0], 0.0, -1.0, ALU.add, ALU.mult)
                pool.wait_ge(s, L0 * tile + 1)
                pool.tensor_tensor(ln_b[:], ln_a[:, 0, :], minus_half[:], ALU.pow).then_inc(s, 1)
                pool.wait_ge(s, L0 * tile + 2)
                pool.tensor_tensor(ln_c[:], mv[:, 0, :, 1], ln_b[:], ALU.mult).then_inc(s, 1)
                pool.wait_ge(s, L0 * tile + 3)
                pool.tensor_tensor(ln_c[:], ln_c[:], ln_b[:], ALU.mult).then_inc(s, 1)
                settled_on(pool, s, L0 * tile + 4)
                pool.tensor_scalar(ln_a[:, 0, :], ln_c[:], LN_EPS, 1.0, ALU.add, ALU.mult).then_inc(s, 1)
                pool.wait_ge(s, L0 * tile + 5)
                pool.tensor_tensor(ln_d[:], ln_a[:, 0, :], minus_half[:], ALU.pow).then_inc(s, 1)
                pool.wait_ge(s, L0 * tile + 6)
                after(pool, xp_ready, tile - 1)
                pool.tensor_tensor(ratio[:, q, :], ln_a[:, 0, :], ln_d[:], ALU.mult)
                pool.tensor_tensor(rs[:, 0, :], ln_b[:], ln_d[:], ALU.mult).then_inc(s, 1)
                pool.wait_ge(s, L0 * tile + 7)
                pool.tensor_tensor(shift_n[:, 0, :], minus_mean[:, 0, :], rs[:, 0, :],
                                   ALU.mult).then_inc(rs_ready[0], 1)

            def split(n, hi, lo, raw):
                pool.wait_ge(split_hi, n + 3)
                pool.tensor_tensor(lo[:], raw[:], hi[:].bitcast(F32), ALU.subtract).then_inc(split_rest, 1)

            def scatter(t, q, first, last):
                if not stages(t)[4]:
                    return
                if first == 0:
                    if isinstance(t, int) and t == NT + 2:
                        pool.wait_ge(area_cleared, 16 * (LIST_ROWS - OVERFLOW) // BLOCK)
                    settled_on(pool, slot_ready, t - 2)
                for n in range(first, last):
                    pool.indirect_dma_start(
                        lists, bass.IndirectOffsetOnAxis(ap=slot[:, q, n:n + 1], axis=0),
                        rows[:, q, n // TOPK, :], None).then_inc(scattered[q], 16)

            def step(t, p, pair):
                has_t, has_u, has_v, has_next, _ = stages(t)
                U, V = t - 1, t - 2
                if isinstance(t, int) and t == 0:
                    ln0_scale(t, 0)
                if has_u:
                    ln_scale(1, U)
                    if isinstance(t, int) and U == 0:
                        split(1, wr_hi, wr_lo, raw_r)
                        split(2, wv_hi, wv_lo, raw_v)
                    pool.wait_ge(xn2_ready, U + 1)
                    pool.wait_ge(xn2_last_ready, U + 1)
                    pool.tensor_tensor(xp[:, 1 - p], xp[:, 1 - p], x_sb[:, 1 - p], ALU.add).then_inc(xx_ready, 1)
                scatter(t, 1 - p, 0, 2)
                if has_v:
                    ln_scale(2, V)
                if has_t:
                    for m in range(KD):
                        settled_on(pool, den_ready, 2 * t + m + 1)
                        pool.tensor_scalar(u[:, m, :], den[:, m, :], WKV_EPS, 2.0, ALU.add,
                                           ALU.mult).then_inc(den2_ready, 1)
                scatter(t, 1 - p, 2, 4)
                if has_next:
                    ln0_scale(t + 1, 1 - p)
                scatter(t, 1 - p, 4, 10)
                if has_t:
                    for m in range(KD):
                        pool.wait_ge(thn_ready, 2 * t + m + 1)
                        pool.wait_ge(rden_ready, 2 * t + m + 1)
                        pool.tensor_tensor(th_r[:, m, :], th_r[:, m, :], u[:, m, :],
                                           ALU.mult).then_inc(yprod_ready, 1)
                scatter(t, 1 - p, 10, 16)
                if isinstance(t, int) and t == 0:
                    split(0, wk_hi, wk_lo, raw_k)
                if has_v:
                    pool.wait_ge(place_ready, V + 1)
                    if isinstance(t, int) and V == NT - 1:
                        pool.wait_ge(over_done, 1)
                    pool.tensor_tensor(chosen[:].rearrange("p (j k) e -> p j k e", j=J),
                                       chosen[:].rearrange("p (j k) e -> p j k e", j=J),
                                       place[:].unsqueeze(2).broadcast_to([P, J, TOPK, E]),
                                       ALU.mult).then_inc(placed_ready, 1)

            run(pool, step)
            for done in scattered:
                pool.wait_ge(done, 16 * NT // 2 * J * TOPK)


def expert_phase(nc, scope, sem, g):
    ident, plan_ready = g["ident"], g["plan_ready"]
    plan_expert, plan_row, plan_mark = g["plan_expert"], g["plan_row"], g["plan_mark"]
    lists, expert_rows = g["lists"], g["expert_rows"]

    def sb(name, shape, dt=F32):
        return scope.enter_context(nc.sbuf_tensor(name, shape, dt))

    def sems(name, n):
        return [sem(f"{name}_{i}") for i in range(n)]

    w = g["experts_w"]
    SLOTS = RING // 2
    keys = sb("keys", [P, SLOTS, 2, KD * DE], F32R)
    xr = sb("xr", [P, SLOTS, SUB, ROW])
    xt_hi, xt_lo = (sb(f"xt_{h}", [P, 2, KD, BLOCK], F32R) for h in ("hi", "lo"))
    h_hi, h_lo = (sb(f"h_{h}", [P, 2, BLOCK], F32R) for h in ("hi", "lo"))
    mark = sb("mark", [P, SUB, TOPK])
    dest = sb("dest", [P, RING, SUB], U32)
    y = sb("y", [P, RING, SUB, D])
    ps = scope.enter_context(nc.psum_tensor("ps2", [P, 8, 512], F32))
    XT, H, Y = 0, 2, 4

    rows_loaded = sems("rows_loaded", SLOTS)
    sent = sems("sent", RING)
    (xt_done, keys_ready, h_done, y_done, xhi_ready, x_ready, hhi_ready, h_ready, ycopy_ready, mark_ready,
     dest_ready) = (sem(n) for n in ("xt_done keys_ready h_done y_done xhi_ready x_ready hhi_ready "
                                     "h_ready ycopy_ready mark_ready dest_ready").split())

    def loop(eng, step, drain=0):
        for i in range(RING):
            step(i, i, 0)
        with eng.Fori(1, NBLOCKS // RING) as ring:
            for r in range(RING):
                step(RING * ring + r, r, ring)
        for i in range(NBLOCKS, NBLOCKS + drain):
            step(i, i % RING, i // RING)

    def settled_on(eng, s, n, also=None):
        if isinstance(n, int):
            eng.wait_ge(s, n)
            if also:
                eng.wait_ge(also, n)
        else:
            with eng.register() as value:
                eng.reg_mov(value, n)
                eng.wait_ge(plan_ready, 1)
                eng.wait_ge(s, value)
                if also:
                    eng.wait_ge(also, value)

    with nc.Block() as block:
        @block.sync
        def _(sp):
            def step(i, r, ring):
                after(sp, xt_done, i - SLOTS + 1)
                after(sp, mark_ready, i - SLOTS + 1)
                row = sp.value_load(plan_row[0:1, bass.ds(i, 1)], min_val=0, max_val=LIST_ROWS - BLOCK)
                sp.dma_start(xr[:, r % SLOTS], lists[bass.ds(row, BLOCK), :].rearrange("(p s) c -> p s c", p=P)
                             ).then_inc(rows_loaded[r % SLOTS], 16)

            loop(sp, step)
            sp.dma_start(g["resid_head"][:], g["residual"][0:HEAD * P, :].rearrange("(g p) d -> p g d", p=P)
                         ).then_inc(g["resid_head_loaded"], 16)
            sp.wait_ge(g["resid_head_loaded"], 16)

        @block.tensor
        def _(pe):
            def step(i, r, ring):
                if not isinstance(i, int) or i < NBLOCKS:
                    pe.wait_ge(rows_loaded[r % SLOTS], 16 * (2 * ring + r // SLOTS + 1))
                    after(pe, x_ready, i - 1)
                    for k in range(KD):
                        for s in range(SUB):
                            mm = pe.transpose(ps[:, XT + r % 2, k * BLOCK + s * P:k * BLOCK + (s + 1) * P],
                                              xr[:, r % SLOTS, s, k * P:(k + 1) * P], ident)
                    mm.then_inc(xt_done, 1)
                if not isinstance(i, int) or i >= 2:
                    e = pe.value_load(plan_expert[0:1, bass.ds(i - 2, 1)], min_val=0, max_val=E - 1)
                q = (r - 1) % 2
                if not isinstance(i, int) or 1 <= i <= NBLOCKS:
                    pe.wait_ge(keys_ready, i)
                    pe.wait_ge(x_ready, i)
                    after(pe, h_ready, i - 2)
                    n = 0
                    for k in range(KD):
                        for half, m in ((0, xt_hi), (0, xt_lo), (1, xt_hi)):
                            mm = pe.matmul(ps[:, H + q, 0:BLOCK],
                                           keys[:, (r - 1) % SLOTS, half, k * DE:(k + 1) * DE],
                                           m[:, q, k, :], start=n == 0, stop=n == 3 * KD - 1)
                            n += 1
                    mm.then_inc(h_done, 1)
                q = (r - 2) % 2
                if not isinstance(i, int) or i >= 2:
                    pe.wait_ge(h_ready, i - 1)
                    after(pe, ycopy_ready, i - 3)
                    v_hi, v_lo = (w[:, h, bass.ds(e, 1), KD * DE:].rearrange("p a w -> p (a w)") for h in (0, 1))
                    for s in range(SUB):
                        cols = ps[:, Y + q, s * D:(s + 1) * D]
                        c = slice(s * P, (s + 1) * P)
                        pe.matmul(cols, h_hi[:, q, c], v_hi, start=True, stop=False)
                        pe.matmul(cols, h_hi[:, q, c], v_lo, start=False, stop=False)
                        mm = pe.matmul(cols, h_lo[:, q, c], v_hi, start=False, stop=True)
                    mm.then_inc(y_done, 1)

            loop(pe, step, drain=2)

        @block.scalar
        def _(act):
            def step(i, r, ring):
                q = r % 2
                if not isinstance(i, int) or i < NBLOCKS:
                    act.wait_ge(xt_done, i + 1)
                    after(act, h_done, i - 1)
                    act.activation(xt_hi[:, q].rearrange("p k b -> p (k b)"), ps[:, XT + q, :],
                                   ACT.Copy).then_inc(xhi_ready, 1)
                q = (r - 1) % 2
                if not isinstance(i, int) or 1 <= i <= NBLOCKS:
                    act.wait_ge(h_done, i)
                    after(act, y_done, i - 2)
                    act.activation(h_hi[:, q, :], ps[:, H + q, 0:BLOCK], ACT.Relu).then_inc(hhi_ready, 1)
                q = (r - 2) % 2
                if not isinstance(i, int) or i >= 2:
                    b = (r - 2) % RING
                    act.wait_ge(y_done, i - 1)
                    after(act, sent[b], 16 * SUB * (ring - 1 if r >= 2 else ring - 2) + 16 * SUB)
                    act.activation(y[:, b].rearrange("p s d -> p (s d)"), ps[:, Y + q, :],
                                   ACT.Copy).then_inc(ycopy_ready, 1)

            loop(act, step, drain=2)

        @block.vector
        def _(dve):
            expert = {}

            def load_expert(i, r):
                expert[r] = dve.value_load(plan_expert[0:1, bass.ds(i, 1)], min_val=0, max_val=E - 1)

            def step(i, r, ring):
                q, qh = r % 2, (r - 1) % 2
                a_block = not isinstance(i, int) or i < NBLOCKS
                if a_block:
                    if r == 0:
                        load_expert(i, r)
                    after(dve, h_done, i - SLOTS + 1)
                    dve.tensor_copy(keys[:, r % SLOTS], w[:, :, bass.ds(expert[r], 1), 0:KD * DE].rearrange(
                        "p h a w -> p (h a) w").bitcast(F32)).then_inc(keys_ready, 1)
                    dve.wait_ge(rows_loaded[r % SLOTS], 16 * (2 * ring + r // SLOTS + 1))
                    after(dve, dest_ready, i)
                    dve.tensor_scalar(mark[:], xr[:, r % SLOTS, :, D:ROW], plan_mark[:, bass.ds(i, 1)], None,
                                      ALU.subtract).then_inc(mark_ready, 1)
                    dve.wait_ge(xhi_ready, i + 1)
                    dve.tensor_tensor(xt_lo[:, q].rearrange("p k b -> p (k b)"), ps[:, XT + q, :],
                                      xt_hi[:, q].rearrange("p k b -> p (k b)").bitcast(F32),
                                      ALU.subtract).then_inc(x_ready, 1)
                    if r < RING - 1:
                        load_expert(i + 1, r + 1)
                if not isinstance(i, int) or 1 <= i <= NBLOCKS:
                    dve.wait_ge(hhi_ready, i)
                    dve.scalar_tensor_tensor(h_lo[:, qh, :], ps[:, H + qh, 0:BLOCK], 0.0,
                                             h_hi[:, qh, :].bitcast(F32), ALU.max, ALU.subtract
                                             ).then_inc(h_ready, 1)
                if a_block:
                    after(dve, sent[r], 16 * SUB * ring)
                    dve.wait_ge(mark_ready, i + 1)
                    dve.tensor_reduce(dest[:, r, :], mark[:], AX_X, ALU.min,
                                      apply_absolute_value=True).then_inc(dest_ready, 1)

            loop(dve, step, drain=1)

        @block.gpsimd
        def _(pool):
            def step(i, r, ring):
                settled_on(pool, ycopy_ready, i + 1, dest_ready)
                for s in range(SUB):
                    pool.indirect_dma_start(
                        expert_rows, bass.IndirectOffsetOnAxis(ap=dest[:, r, s:s + 1], axis=0), y[:, r, s, :],
                        None, bounds_check=OUT_ROWS - 1, oob_is_err=False).then_inc(sent[r], 16)

            loop(pool, step)
            for r in range(RING):
                pool.wait_ge(sent[r], 16 * SUB * NBLOCKS // RING)


def combine_phase(nc, scope, sem, g):
    gates, expert_rows, residual, out = g["gates"], g["expert_rows"], g["residual"], g["out"]
    GROUPS = 2
    STEPS = N // P // GROUPS
    DEPTH = 4
    ye = scope.enter_context(nc.sbuf_tensor("ye", [P, DEPTH, GROUPS, TOPK, D], F32))
    resid = scope.enter_context(nc.sbuf_tensor("resid", [P, DEPTH, GROUPS, D], F32))
    ye_loaded = [sem(f"ye_loaded_{r}") for r in range(DEPTH)]
    stored = [sem(f"stored_{r}") for r in range(DEPTH)]
    resid_loaded = [sem(f"resid_loaded_{r}") for r in range(DEPTH)]
    sum_step = sem("sum_step")
    ADDS = TOPK * GROUPS
    HEAD_RINGS = HEAD // GROUPS // DEPTH
    assert HEAD % (GROUPS * DEPTH) == 0

    def sum_of(i, r, head):
        return g["resid_head"][:, bass.ds(i * GROUPS, GROUPS), :] if head else resid[:, r]

    with nc.Block() as block:
        def loop(eng, step):
            for i in range(DEPTH):
                step(i, i, 0, True)
            with eng.Fori(1, HEAD_RINGS) as ring:
                for r in range(DEPTH):
                    step(DEPTH * ring + r, r, ring, True)
            with eng.Fori(HEAD_RINGS, STEPS // DEPTH) as ring:
                for r in range(DEPTH):
                    step(DEPTH * ring + r, r, ring, False)

        @block.sync
        def _(sp):
            def step(i, r, ring, head):
                tokens = GROUPS * P
                after(sp, sum_step, ADDS * (i - DEPTH + 1))
                sp.dma_start(ye[:, r], expert_rows[bass.ds(i * (tokens * TOPK), tokens * TOPK), :]
                             .rearrange("(g p k) d -> p g k d", p=P, k=TOPK)).then_inc(ye_loaded[r], 16)
                if not head:
                    after(sp, stored[r], 16 * ring)
                    sp.dma_start(resid[:, r], residual[bass.ds(i * tokens, tokens), :]
                                 .rearrange("(g p) d -> p g d", p=P)).then_inc(resid_loaded[r], 16)

            loop(sp, step)

        @block.vector
        def _(dve):
            def step(i, r, ring, head):
                dve.wait_ge(ye_loaded[r], 16 * (ring + 1))
                if not head:
                    dve.wait_ge(resid_loaded[r], 16 * (ring - HEAD_RINGS + 1))
                for k in range(TOPK):
                    for j in range(GROUPS):
                        if k > 0:
                            dve.wait_ge(sum_step, ADDS * i + (k - 1) * GROUPS + j + 1)
                        acc = sum_of(i, r, head)[:, j, :]
                        dve.scalar_tensor_tensor(
                            acc, ye[:, r, j, k, :],
                            gates[:, bass.ds(i * GROUPS + j, 1), k:k + 1].rearrange("p a b -> p (a b)"),
                            acc, ALU.mult, ALU.add).then_inc(sum_step, 1)

            loop(dve, step)

        @block.scalar
        def _(act):
            def step(i, r, ring, head):
                act.wait_ge(sum_step, ADDS * (i + 1))
                act.dma_start(out[bass.ds(i * (GROUPS * P), GROUPS * P), :].rearrange("(g p) d -> p g d", p=P),
                              sum_of(i, r, head)).then_inc(stored[r], 16)

            loop(act, step)
            for r in range(DEPTH):
                act.wait_ge(stored[r], 16 * STEPS // DEPTH)


def kernel(**inputs):
    import concourse.bacc as bacc
    from concourse.bass_utils import run_bass_kernel_spmd

    a = {n.removeprefix("L0_attn_").removeprefix("L0_ffn_"): np.asarray(v) for n, v in inputs.items()}

    def rows_first(w, k):
        return w.T.reshape(k, P, -1).transpose(1, 0, 2)

    consts = np.zeros((P, C_END), np.float32)
    p = np.arange(P)
    consts[:, C_IDENT:C_IDENT + P] = np.eye(P)
    consts[:, C_TRI:C_TRI + P] = p[:, None] < p[None, :]
    consts[:, C_EXPERT:C_EXPERT + E] = np.arange(E)
    consts[:, C_LIST:C_LIST + E] = np.arange(E) * LIST
    consts[:, C_OUTROW:C_OUTROW + J * TOPK] = ((np.arange(J)[None, :, None] * P + p[:, None, None]) * TOPK
                                              + np.arange(TOPK) + SPACED).reshape(P, -1)
    consts[:, C_BLOCK:C_END] = np.arange(NBLOCKS)
    laid = {
        "x": a["x"].reshape(N, D),
        "w_time": np.stack([rows_first(a[n], KD) for n in ("Ww", "Wr", "Wk", "Wv")], axis=1),
        "w_out": rows_first(a["Wo"], KD),
        "w_rec": rows_first(a["Wrec"], KD),
        "w_key": rows_first(a["Wkey"], KD),
        "w_val": rows_first(a["Wval"], KF),
        "ln_params": np.stack([a[n].reshape(KD, P).T for n in ("ln1_g", "ln1_b", "ln2_g", "ln2_b")], axis=1),
        "decay_in": a["time_decay"].reshape(KD, P).T,
        "sel_in": rows_first(a["expert_sel"], KD),
        "expert_in": np.concatenate([a["keys"].reshape(E, KD, P, DE).transpose(2, 0, 1, 3).reshape(P, E, KD * DE),
                                     a["values"].transpose(1, 0, 2)], axis=2),
        "consts_in": consts,
    }
    nc = bacc.Bacc("TRN2", target_bir_lowering=False, num_devices=1)
    arrays, args = {}, {}
    for name, v in laid.items():
        arrays[f"in_{name}"] = np.ascontiguousarray(v)
        args[name] = nc.dram_tensor(f"in_{name}", v.shape, mybir.dt.from_np(v.dtype), kind="ExternalInput").ap()
    args["out"] = nc.dram_tensor("out_dram", (N, D), F32, kind="ExternalOutput").ap()
    args["lists"] = nc.dram_tensor("lists", (LIST_ROWS, ROW), F32, kind="Internal").ap()
    args["expert_rows"] = nc.dram_tensor("expert_rows", (N * TOPK, D), F32, kind="Internal").ap()
    args["residual"] = nc.dram_tensor("residual", (N, D), F32, kind="Internal").ap()
    program(nc, **args)
    r = run_bass_kernel_spmd(nc, [arrays], core_ids=[0])
    return r.results[0]["out_dram"].reshape(B, S, D)
```
